# Optimizing a Trainium2 kernel written in Bass

```python
import numpy as np
import jax
import jax.numpy as jnp

def _softmax(x, axis=-1):
    return jax.nn.softmax(x, axis=axis)

def _gelu(x):
    return jax.nn.gelu(x, approximate=True)

def _silu(x):
    return jax.nn.silu(x)

def _sigmoid(x):
    return jax.nn.sigmoid(x)

def _layernorm(x, axis=-1, eps=1e-05):
    m = jnp.mean(x, axis=axis, keepdims=True)
    v = jnp.var(x, axis=axis, keepdims=True)
    return (x - m) / jnp.sqrt(v + eps)

def _scatter_add(tgt, idx, src, axis=0):
    return tgt.at[idx].add(src)

def _segment_sum(src, seg, n):
    return jax.ops.segment_sum(src, seg, n)
kernel_name = 'mk_sandwich_d1_jaxref_r8_81556a'

def setup_inputs(seed: int=0):
    np.random.seed(seed)
    _w = jnp.asarray

    def _L0_attn_setup():
        import jax, jax.numpy as jnp
        import numpy as np
        D_MODEL = 512
        D_XB = 128
        D_INNER = 512
        HEADDIM = 128
        DSTATE = 128
        NHEADS = D_INNER // HEADDIM
        DCONV = 4
        INTER = 1792
        EPS = 1e-05
        CHUNK = 128

        def rmsnorm(x, w):
            return x * jax.lax.rsqrt(jnp.mean(x * x, axis=-1, keepdims=True) + EPS) * w

        def silu(x):
            return x * jax.nn.sigmoid(x)

        def mamba2(x, w_in, conv_w, conv_b, A_log, D, dt_bias, w_out):
            B, L, _ = x.shape
            H, P, N = (NHEADS, HEADDIM, DSTATE)
            G = D_XB // P
            rep = H // G
            zxbcdt = x @ w_in.T
            z, xs, Bs, Cs, dt = jnp.split(zxbcdt, [D_INNER, D_INNER + D_XB, D_INNER + 2 * D_XB, 2 * D_INNER + 2 * D_XB], axis=-1)
            xBC = jnp.concatenate([xs, Bs, Cs], axis=-1)
            conv = jax.lax.conv_general_dilated(xBC.transpose(0, 2, 1), conv_w[:, None, :], (1,), [(DCONV - 1, 0)], feature_group_count=conv_w.shape[0])
            xBC = silu(conv.transpose(0, 2, 1) + conv_b)
            xs, Bs, Cs = jnp.split(xBC, [D_XB, 2 * D_XB], axis=-1)
            dt = jax.nn.softplus(dt + dt_bias)
            A = -jnp.exp(A_log)
            xh = jnp.repeat(xs.reshape(B, L, G, P), rep, axis=2)
            Bh = jnp.repeat(Bs.reshape(B, L, G, N), rep, axis=2)
            Ch = Cs.reshape(B, L, H, N)
            c, Q = (L // CHUNK, CHUNK)
            a = (dt * A).reshape(B, c, Q, H).transpose(0, 1, 3, 2)
            dtc = dt.reshape(B, c, Q, H).transpose(0, 1, 3, 2)
            Xc = xh.reshape(B, c, Q, H, P).transpose(0, 1, 3, 2, 4)
            Bc = Bh.reshape(B, c, Q, H, N).transpose(0, 1, 3, 2, 4)
            Cc = Ch.reshape(B, c, Q, H, N).transpose(0, 1, 3, 2, 4)
            cs = jnp.cumsum(a, axis=-1)
            tri = jnp.tril(jnp.ones((Q, Q), bool))
            Ldec = jnp.where(tri, jnp.exp(cs[..., :, None] - cs[..., None, :]), 0.0)
            Xdt = Xc * dtc[..., None]
            att = jnp.einsum('bchqn,bchkn->bchqk', Cc, Bc) * Ldec
            Yd = jnp.einsum('bchqk,bchkp->bchqp', att, Xdt)
            dec_end = jnp.exp(cs[..., -1:] - cs)
            states = jnp.einsum('bchq,bchqn,bchqp->bchpn', dec_end, Bc, Xdt)
            g = jnp.exp(cs[..., -1])

            def step(S, inp):
                gk, st = inp
                return (gk[:, :, None, None] * S + st, S)
            S0 = jnp.zeros((B, H, P, N), x.dtype)
            _, prev = jax.lax.scan(step, S0, (g.transpose(1, 0, 2), states.transpose(1, 0, 2, 3, 4)))
            prev = prev.transpose(1, 0, 2, 3, 4)
            Yo = jnp.einsum('bchqn,bchpn,bchq->bchqp', Cc, prev, jnp.exp(cs))
            Y = (Yd + Yo).transpose(0, 1, 3, 2, 4).reshape(B, L, H, P)
            Y = Y + D[:, None] * xh
            y = Y.reshape(B, L, D_INNER) * silu(z)
            return y @ w_out.T
        key = jax.random.key(seed)
        ks = jax.random.split(key, 10)
        B, L = (2, 256)
        proj_out = 2 * D_INNER + 2 * D_XB + NHEADS
        conv_dim = 2 * D_XB + D_INNER
        return {'hidden_states': jax.random.normal(ks[0], (B, L, D_MODEL), jnp.float32), 'w_in': jax.random.normal(ks[1], (proj_out, D_MODEL), jnp.float32) * 0.02, 'conv_w': jax.random.normal(ks[2], (conv_dim, DCONV), jnp.float32) * 0.1, 'conv_b': jnp.zeros((conv_dim,), jnp.float32), 'A_log': jnp.log(jnp.arange(1, NHEADS + 1, dtype=jnp.float32)), 'D': jnp.ones((NHEADS,), jnp.float32), 'dt_bias': jax.random.normal(ks[3], (NHEADS,), jnp.float32) * 0.1, 'w_out': jax.random.normal(ks[4], (D_MODEL, D_INNER), jnp.float32) * 0.02, 'ln1_w': jnp.ones((D_MODEL,), jnp.float32), 'ln2_w': jnp.ones((D_MODEL,), jnp.float32), 'gate_w': jax.random.normal(ks[5], (INTER, D_MODEL), jnp.float32) * 0.02, 'up_w': jax.random.normal(ks[6], (INTER, D_MODEL), jnp.float32) * 0.02, 'down_w': jax.random.normal(ks[7], (D_MODEL, INTER), jnp.float32) * 0.02}
    _L0_attn_in = _L0_attn_setup()

    def _L0_ffn_setup():
        import jax, jax.numpy as jnp
        import numpy as np
        NUM_EXPERTS = 4
        HIDDEN = 512
        RANK = 8
        ALPHA = 8.0
        SCALE = ALPHA / RANK
        key = jax.random.key(seed)
        ks = jax.random.split(key, 6)
        B, T, H, E, R = (4, 512, HIDDEN, NUM_EXPERTS, RANK)
        x = jax.random.normal(ks[0], (B, T, H), dtype=jnp.float32)
        W_up = jax.random.normal(ks[1], (H, H), dtype=jnp.float32) / np.sqrt(H)
        gate_w = jax.random.normal(ks[2], (E, H), dtype=jnp.float32) / np.sqrt(H)
        expert_bias = jnp.zeros((E,), dtype=jnp.float32)
        lora_A = jax.random.normal(ks[3], (E, R, H), dtype=jnp.float32) / np.sqrt(H)
        lora_B = jax.random.normal(ks[4], (E, H, R), dtype=jnp.float32) * 0.01
        return {'x': x, 'W_up': W_up, 'gate_w': gate_w, 'expert_bias': expert_bias, 'lora_A': lora_A, 'lora_B': lora_B}
    _L0_ffn_in = _L0_ffn_setup()
    _d = {'L0_attn_hidden_states': _L0_attn_in['hidden_states'], 'L0_attn_w_in': _L0_attn_in['w_in'], 'L0_attn_conv_w': _L0_attn_in['conv_w'], 'L0_attn_conv_b': _L0_attn_in['conv_b'], 'L0_attn_A_log': _L0_attn_in['A_log'], 'L0_attn_D': _L0_attn_in['D'], 'L0_attn_dt_bias': _L0_attn_in['dt_bias'], 'L0_attn_w_out': _L0_attn_in['w_out'], 'L0_attn_ln1_w': _L0_attn_in['ln1_w'], 'L0_attn_ln2_w': _L0_attn_in['ln2_w'], 'L0_attn_gate_w': _L0_attn_in['gate_w'], 'L0_attn_up_w': _L0_attn_in['up_w'], 'L0_attn_down_w': _L0_attn_in['down_w'], 'L0_ffn_W_up': _L0_ffn_in['W_up'], 'L0_ffn_gate_w': _L0_ffn_in['gate_w'], 'L0_ffn_expert_bias': _L0_ffn_in['expert_bias'], 'L0_ffn_lora_A': _L0_ffn_in['lora_A'], 'L0_ffn_lora_B': _L0_ffn_in['lora_B']}
    _x0 = _d['L0_attn_hidden_states']
    _d['L0_attn_hidden_states'] = jax.random.normal(jax.random.fold_in(jax.random.key(seed), 1), (8, 256, 512), dtype=_x0.dtype)
    del _x0
    return _d

def reference(L0_attn_hidden_states, L0_attn_w_in, L0_attn_conv_w, L0_attn_conv_b, L0_attn_A_log, L0_attn_D, L0_attn_dt_bias, L0_attn_w_out, L0_attn_ln1_w, L0_attn_ln2_w, L0_attn_gate_w, L0_attn_up_w, L0_attn_down_w, L0_ffn_W_up, L0_ffn_gate_w, L0_ffn_expert_bias, L0_ffn_lora_A, L0_ffn_lora_B):

    def _L0_attn_ref(hidden_states, w_in, conv_w, conv_b, A_log, D, dt_bias, w_out, ln1_w, ln2_w, gate_w, up_w, down_w):
        import jax, jax.numpy as jnp
        import numpy as np
        D_MODEL = 512
        D_XB = 128
        D_INNER = 512
        HEADDIM = 128
        DSTATE = 128
        NHEADS = D_INNER // HEADDIM
        DCONV = 4
        INTER = 1792
        EPS = 1e-05
        CHUNK = 128

        def rmsnorm(x, w):
            return x * jax.lax.rsqrt(jnp.mean(x * x, axis=-1, keepdims=True) + EPS) * w

        def silu(x):
            return x * jax.nn.sigmoid(x)

        def mamba2(x, w_in, conv_w, conv_b, A_log, D, dt_bias, w_out):
            B, L, _ = x.shape
            H, P, N = (NHEADS, HEADDIM, DSTATE)
            G = D_XB // P
            rep = H // G
            zxbcdt = x @ w_in.T
            z, xs, Bs, Cs, dt = jnp.split(zxbcdt, [D_INNER, D_INNER + D_XB, D_INNER + 2 * D_XB, 2 * D_INNER + 2 * D_XB], axis=-1)
            xBC = jnp.concatenate([xs, Bs, Cs], axis=-1)
            conv = jax.lax.conv_general_dilated(xBC.transpose(0, 2, 1), conv_w[:, None, :], (1,), [(DCONV - 1, 0)], feature_group_count=conv_w.shape[0])
            xBC = silu(conv.transpose(0, 2, 1) + conv_b)
            xs, Bs, Cs = jnp.split(xBC, [D_XB, 2 * D_XB], axis=-1)
            dt = jax.nn.softplus(dt + dt_bias)
            A = -jnp.exp(A_log)
            xh = jnp.repeat(xs.reshape(B, L, G, P), rep, axis=2)
            Bh = jnp.repeat(Bs.reshape(B, L, G, N), rep, axis=2)
            Ch = Cs.reshape(B, L, H, N)
            c, Q = (L // CHUNK, CHUNK)
            a = (dt * A).reshape(B, c, Q, H).transpose(0, 1, 3, 2)
            dtc = dt.reshape(B, c, Q, H).transpose(0, 1, 3, 2)
            Xc = xh.reshape(B, c, Q, H, P).transpose(0, 1, 3, 2, 4)
            Bc = Bh.reshape(B, c, Q, H, N).transpose(0, 1, 3, 2, 4)
            Cc = Ch.reshape(B, c, Q, H, N).transpose(0, 1, 3, 2, 4)
            cs = jnp.cumsum(a, axis=-1)
            tri = jnp.tril(jnp.ones((Q, Q), bool))
            Ldec = jnp.where(tri, jnp.exp(cs[..., :, None] - cs[..., None, :]), 0.0)
            Xdt = Xc * dtc[..., None]
            att = jnp.einsum('bchqn,bchkn->bchqk', Cc, Bc) * Ldec
            Yd = jnp.einsum('bchqk,bchkp->bchqp', att, Xdt)
            dec_end = jnp.exp(cs[..., -1:] - cs)
            states = jnp.einsum('bchq,bchqn,bchqp->bchpn', dec_end, Bc, Xdt)
            g = jnp.exp(cs[..., -1])

            def step(S, inp):
                gk, st = inp
                return (gk[:, :, None, None] * S + st, S)
            S0 = jnp.zeros((B, H, P, N), x.dtype)
            _, prev = jax.lax.scan(step, S0, (g.transpose(1, 0, 2), states.transpose(1, 0, 2, 3, 4)))
            prev = prev.transpose(1, 0, 2, 3, 4)
            Yo = jnp.einsum('bchqn,bchpn,bchq->bchqp', Cc, prev, jnp.exp(cs))
            Y = (Yd + Yo).transpose(0, 1, 3, 2, 4).reshape(B, L, H, P)
            Y = Y + D[:, None] * xh
            y = Y.reshape(B, L, D_INNER) * silu(z)
            return y @ w_out.T
        res = hidden_states
        h = rmsnorm(hidden_states, ln1_w)
        h = res + mamba2(h, w_in, conv_w, conv_b, A_log, D, dt_bias, w_out)
        res = h
        h2 = rmsnorm(h, ln2_w)
        mlp = silu(h2 @ gate_w.T) * (h2 @ up_w.T) @ down_w.T
        return res + mlp

    def _L0_ffn_ref(x, W_up, gate_w, expert_bias, lora_A, lora_B):
        import jax, jax.numpy as jnp
        import numpy as np
        NUM_EXPERTS = 4
        HIDDEN = 512
        RANK = 8
        ALPHA = 8.0
        SCALE = ALPHA / RANK
        B, T, H = x.shape
        E = gate_w.shape[0]
        x_flat = x.reshape(-1, H)
        logits = x_flat @ gate_w.T + expert_bias
        top1 = jnp.argmax(logits, axis=-1)
        one_hot = jax.nn.one_hot(top1, E, dtype=x_flat.dtype)
        base_out = jnp.einsum('bth,oh->bto', x, W_up)
        z = jnp.einsum('nh,erh->ner', x_flat, lora_A)
        d = jnp.einsum('ner,ehr->neh', z, lora_B) * SCALE
        delta = jnp.einsum('neh,ne->nh', d, one_hot)
        return base_out + delta.reshape(B, T, H)
    x = L0_attn_hidden_states
    x = x + _layernorm(_L0_attn_ref(_layernorm(x, axis=-1), L0_attn_w_in, L0_attn_conv_w, L0_attn_conv_b, L0_attn_A_log, L0_attn_D, L0_attn_dt_bias, L0_attn_w_out, L0_attn_ln1_w, L0_attn_ln2_w, L0_attn_gate_w, L0_attn_up_w, L0_attn_down_w), axis=-1)
    x = x + _layernorm(_L0_ffn_ref(_layernorm(x, axis=-1), L0_ffn_W_up, L0_ffn_gate_w, L0_ffn_expert_bias, L0_ffn_lora_A, L0_ffn_lora_B), axis=-1)
    return x

_drawn_inputs = setup_inputs


def setup_inputs(seed=0):
    import zlib

    import numpy as np

    out = dict(_drawn_inputs(seed))
    spreads = {'L0_attn_conv_b': (0.0, 0.8),
     'L0_attn_D': (1.0, 0.6),
     'L0_attn_ln1_w': (1.0, 0.6),
     'L0_attn_ln2_w': (1.0, 0.6),
     'L0_ffn_expert_bias': (0.0, 0.8)}
    factors = {'L0_attn_w_in': 8.0,
     'L0_attn_conv_w': 8.0,
     'L0_attn_A_log': 8.0,
     'L0_attn_dt_bias': 8.0,
     'L0_attn_w_out': 8.0,
     'L0_ffn_gate_w': 5.497,
     'L0_ffn_lora_A': 4.715,
     'L0_ffn_lora_B': 4.703,
     'L0_attn_gate_w': 64.0,
     'L0_attn_up_w': 64.0,
     'L0_attn_down_w': 64.0}
    for name, (base, spread) in spreads.items():
        noise = np.random.default_rng([zlib.crc32(name.encode()), seed]).standard_normal(out[name].shape)
        drawn = base * np.exp(spread * noise) if base else spread * noise
        out[name] = jnp.asarray(drawn.astype(out[name].dtype))
    for name, factor in factors.items():
        out[name] = (out[name] * factor).astype(out[name].dtype)
    return out
```

```python
from contextlib import ExitStack

import concourse.bass as bass
from concourse import mybir

F32 = mybir.dt.float32
F16 = mybir.dt.float16
BF16 = mybir.dt.bfloat16
I32 = mybir.dt.int32
ALU = mybir.AluOpType
ACT = mybir.ActivationFunctionType
AX = mybir.AxisListType
RMAX = bass.bass_isa.ReduceOp.max
RADD = bass.bass_isa.ReduceOp.add

P = 128
D = 512
KB = D // P
SEQ = 256
TILES = SEQ // P
GROUPS = 8
H = 4
TAPS = 4
FBLK = 14
XBC = 6
E = 4
R = 8
EPS = 1e-5

U_IN, U_OUT, U_GATE, U_UP, U_DOWN, U_LIN, UNITS = 0, 10, 14, 28, 42, 56, 60

ROOT_D = 22.63
ACT_SCALE = 64.0
TOP = 30000.0
BF_SLACK = 1.02
SERIES = 1.0 / 64
TINY = 1e-36
POW2 = 0x7F800000


class Chain:

    def __init__(self, eng, sem, per, wait=None):
        self.eng, self.sem, self.per, self.wait = eng, sem, per, wait or eng.wait_ge

    def group(self, g):
        self.g, self.k = g, 0

    def __call__(self, ins, wait=True):
        self.k += 1
        ins.then_inc(self.sem, 1)
        if wait:
            self.wait(self.sem, self.g * self.per + self.k)

    def close(self):
        assert self.k == self.per, (self.sem, self.k)


def build(nc, x, w_in, w_dt, w_out, w_gate, w_up, w_down, w_lin, w_gl, lora_b, cols, rows, ln_rows, out):
    x_g = x.rearrange("(g t p) d -> g p t d", t=TILES, p=P)
    out_g = out.rearrange("(g t p) d -> g p t d", t=TILES, p=P)
    ctx = ExitStack()
    with ctx:
        def sb(name, shape, dt=F32):
            return ctx.enter_context(nc.sbuf_tensor(name, shape, dt))

        def ps(name):
            return ctx.enter_context(nc.psum_tensor(name, [P, 512], F32))

        made = {}

        def sem(name):
            if name not in made:
                made[name] = ctx.enter_context(nc.semaphore(name))
            return made[name]

        W = sb("weights", [P, UNITS, 512])
        Wh = W[:].bitcast(F16).rearrange("p u (s n) -> p u s n", s=2)
        dt_raw = sb("dt_raw", [P, KB, H])
        dt_w = sb("dt_w", [P, 2, KB, H], F16)
        gl_raw = sb("gl_raw", [P, KB, E + E * R])
        gl_w = sb("gl_w", [P, 2, KB, E + E * R], F16)
        lorab = sb("lorab", [E * R, D])
        colt = sb("cols_t", [P, 30])
        conv_w, conv_b = colt[:, 0:24], colt[:, 24:30]
        lnt = sb("ln_rows_t", [P, 2, D])
        rowt = sb("rows_t", [P, 16])
        neg_a = sb("neg_a", [P, H])
        cw = sb("conv_ws", [P, XBC * TAPS])
        ident = sb("ident", [P, P])
        tri = sb("tri", [P, P])
        below = sb("below", [P, P])
        ones = sb("ones", [P, P])
        norms = sb("norms", [P, UNITS])
        mabs = sb("mabs", [P, 2, KB])
        sc = sb("scales", [P, 7, 5])
        bound = sb("bound", [P, 10])
        c_half = sb("minus_half", [P, 4])

        xa = sb("xa", [P, TILES, D])
        h01 = sb("h01", [P, TILES, D])
        hn = sb("hn", [P, TILES, D])
        ht = sb("ht", [P, 2, KB, SEQ], F16)
        pad = sb("conv_pad", [P, XBC, TAPS - 1 + SEQ])
        xbc = sb("xbc", [P, XBC, SEQ])
        sz = sb("silu_z", [P, H, SEQ])
        tok = sb("tok", [P, 3, P])
        stats_a = sb("stats_a", [P, TILES, 6])
        mv_a = sb("mv_a", [P, TILES, 2])
        s_a = sb("small_a", [P, 2, TILES])
        dts = sb("dts", [P, 6, TILES, H])
        a_t = sb("a_t", [P, TILES, H])
        ra = sb("ra", [P, TILES, H, P])
        dec = sb("dec", [P, TILES, H, P])
        w0 = sb("w0", [P, H])
        tdt = hn[:].rearrange("p t (h q) -> p t h q", h=H)
        xw = hn[:, 0].rearrange("p (h q) -> p h q", h=H)
        ce = hn[:, 1].rearrange("p (h q) -> p h q", h=H)
        y = sb("y", [P, H, SEQ])
        ss = sb("sumsq", [P, 2, TILES])
        h2t = sb("h2t", [P, 2, KB, SEQ], F16)
        h1b = sb("h1b", [P, TILES, D])
        sg = sb("sg", [P, 2, SEQ])
        act = sb("act", [P, 4, 2, SEQ], F16)
        mlp = sb("mlp", [P, TILES, D])
        x1 = sb("x1", [P, TILES, D])
        h3 = sb("h3", [P, TILES, D])
        h3t = sb("h3t", [P, 2, KB, SEQ], F16)
        scaled_d, scaled_p = mlp, h3
        square = h3t[:].rearrange("p s k q -> p (s k q)").bitcast(F32)
        stats_c = sb("stats_c", [P, TILES, 6])
        mv_c = sb("mv_c", [P, TILES, 2])
        s_c = sb("small_c", [P, TILES])
        lg = sb("logits", [P, TILES, E])
        zs = sb("zs", [P, TILES, E * R])
        mx = sb("mx", [P, TILES])
        eq = sb("eq", [P, TILES, E])
        seen = sb("seen", [P, TILES, E])
        hot = sb("hot", [P, TILES, E])
        zt = sb("zt", [E * R, SEQ])

        GU = [ps("gu0"), ps("gu1")]
        ACC = [ps("acc0"), ps("acc1")]
        WA = [ps("wa0"), ps("wa1"), ps("wa2")]
        WC = ps("wc")

        T_IN, T_GATE, T_UP, T_DOWN, T_LIN, T_GL, T_DT = range(7)
        inv_in, inv_gate, inv_up = sc[:, T_IN, 4:5], sc[:, T_GATE, 4:5], sc[:, T_UP, 4:5]
        inv_lin, inv_gl, inv_dt = sc[:, T_LIN, 4:5], sc[:, T_GL, 4:5], sc[:, T_DT, 4:5]
        act_scale = bound[:, 0:1]
        up_to_act = bound[:, 1:2]
        inv_down = bound[:, 2:3]
        lora_scale = bound[:, 3:4]
        ln_scale = bound[:, 4:6]

        PIECES = [(0, 2), (2, 4), (4, 6), (6, 8), (8, 10), (10, 14)]
        for base in (U_GATE, U_UP, U_DOWN):
            PIECES += [(base + a, min(base + a + 4, base + FBLK)) for a in range(0, FBLK, 4)]
        PIECES += [(U_LIN, UNITS)]
        SOURCES = [(U_IN, w_in), (U_OUT, w_out), (U_GATE, w_gate), (U_UP, w_up), (U_DOWN, w_down),
                   (U_LIN, w_lin)]

        def piece_of(u):
            return next(n for n, (a, b) in enumerate(PIECES) if a <= u < b)

        UNITS_OF = {T_IN: range(U_IN, U_OUT), T_GATE: range(U_GATE, U_UP), T_UP: range(U_UP, U_DOWN),
                    T_DOWN: range(U_DOWN, U_LIN), T_LIN: range(U_LIN, UNITS)}

        def pieces_of(t):
            return sorted({piece_of(u) for u in UNITS_OF[t]})

        def piecewise(t):
            return [("norms", t, n) for n in pieces_of(t)]

        def splits(t, n):
            u = list(UNITS_OF[t])
            return [("split", t, u[i:i + n]) for i in range(0, len(u), n)]

        in_order = {}

        def at(step, f, *jobs):
            in_order.setdefault((step, f), []).extend(jobs)

        at(0, 0, *piecewise(T_IN), ("scale", T_IN, None), ("small", T_DT, None), *splits(T_IN, 10))
        for n, f in enumerate((1, 2, 3, 4)):
            at(0, f, piecewise(T_GATE)[n])
        at(0, 4, ("scale", T_GATE, None))
        for n, f in enumerate((5, 6, 7)):
            at(0, f, splits(T_GATE, 5)[n])
        for n, f in enumerate((6, 7, 8, 9)):
            at(0, f, piecewise(T_UP)[n])
        at(0, 9, ("scale", T_UP, None))
        for n, f in enumerate((10, 11, 12)):
            at(0, f, splits(T_UP, 5)[n])
        at(0, 12, *piecewise(T_DOWN)[0:2])
        at(0, 13, *piecewise(T_DOWN)[2:4], ("scale", T_DOWN, None))
        for n, f in enumerate((0, 1, 2)):
            at(1, f, splits(T_DOWN, 5)[n])
        at(1, 3, *piecewise(T_LIN), ("scale", T_LIN, None))
        at(1, 4, *splits(T_LIN, 4), ("small", T_GL, None))

        order = [u for key in sorted(in_order) for kind, _, us in in_order[key] if kind == "split" for u in us]
        path = {u: "p" if n % 3 == 2 else "d" for n, u in enumerate(order)}
        rank = {u: sum(path[v] == path[u] for v in order[:n]) for n, u in enumerate(order)}
        scale_order = [t for key in sorted(in_order) for kind, t, _ in in_order[key] if kind in ("scale", "small")]
        piece_order = [n for key in sorted(in_order) for kind, _, n in in_order[key] if kind == "norms"]

        def wait_split(eng, units):
            for p, s in (("d", split_d), ("p", split_p)):
                n = max([rank[u] + 1 for u in units if path[u] == p], default=0)
                if n:
                    eng.wait_ge(s, n)

        split_d, split_p, small_split = sem("split_d"), sem("split_p"), sem("small_split")
        s_piece = [sem(f"piece{n}_loaded") for n in range(len(PIECES))]
        small_loaded, lora_loaded = sem("small_loaded"), sem("lora_loaded")
        x_loaded, xc_loaded, stored = sem("x_loaded"), sem("xc_loaded"), sem("stored")
        masks_made = sem("masks_made")
        def prev(g, per, k, eng, s):
            if not (isinstance(g, int) and g == 0):
                eng.wait_ge(s, g * per - per + k)

        block = ctx.enter_context(nc.Block())

        def steps(eng, step):
            step(0, None, None)
            step(1, 0, None)
            step(2, 1, 0)
            with eng.Fori(2, GROUPS - 1) as i:
                step(i + 1, i, i - 1)
            step(None, GROUPS - 1, GROUPS - 2)
            step(None, None, GROUPS - 1)

        @block.sync
        def _(sp):
            def load_piece(n):
                a, b = PIECES[n]
                base, src = max((p for p in SOURCES if p[0] <= a), key=lambda p: p[0])
                v = src[a - base:b - base]
                v = v.rearrange("u p k n -> p u (k n)") if len(src.shape) == 4 else v.rearrange("u p n -> p u n")
                sp.dma_start(W[:, a:b, :], v).then_inc(s_piece[n], 16)

            sp.dma_start(xa[:], x_g[0]).then_inc(x_loaded, 16)
            sp.dma_start(lnt[:].rearrange("p t d -> p (t d)"), ln_rows.broadcast_to([P, 2 * D]))\
                .then_inc(small_loaded, 16)
            sp.dma_start(colt[:], cols).then_inc(small_loaded, 16)
            sp.dma_start(rowt[:], rows.broadcast_to([P, 16])).then_inc(small_loaded, 16)
            sp.dma_start(dt_raw[:], w_dt).then_inc(small_loaded, 16)
            for n in range(len(PIECES)):
                load_piece(n)
            sp.dma_start(gl_raw[:], w_gl).then_inc(lora_loaded, 16)
            sp.dma_start(lorab[:], lora_b).then_inc(lora_loaded, 16)

            def step(a, b, c):
                if a is not None and not (isinstance(a, int) and a == 0):
                    sp.wait_ge(sem("h0_ready"), a * 2)
                    sp.dma_start(xa[:], x_g[a]).then_inc(x_loaded, 16)
                if c is not None:
                    prev(c, 16, 16, sp, stored)
                    sp.dma_start(x1[:], x_g[c]).then_inc(xc_loaded, 16)
                    sp.wait_ge(sem("out_ready"), c * 2 + 2)
                    sp.dma_start(out_g[c], h3[:]).then_inc(stored, 16)

            steps(sp, step)
            sp.wait_ge(stored, 16 * GROUPS)

        @block.gpsimd
        def _(pool):
            nc.gpsimd.memset(ident[:], 0.0).then_inc(masks_made, 1)
            nc.gpsimd.memset(tri[:], 1.0).then_inc(masks_made, 1)
            nc.gpsimd.memset(below[:], 1.0).then_inc(masks_made, 1)
            nc.gpsimd.memset(ones[:], 1.0).then_inc(masks_made, 1)
            nc.gpsimd.memset(pad[:, :, 0:TAPS - 1], 0.0).then_inc(masks_made, 1)
            nc.gpsimd.memset(c_half[:, 0:2], -0.5).then_inc(masks_made, 1)
            nc.gpsimd.memset(c_half[:, 2:4], -1.0).then_inc(masks_made, 1)
            pool.wait_ge(masks_made, 7)
            nc.gpsimd.affine_select(out=ident[:], in_=ident[:], compare_op=ALU.not_equal, fill=1.0, base=0,
                                    pattern=[[-1, P]], channel_multiplier=1).then_inc(masks_made, 1)
            nc.gpsimd.affine_select(out=tri[:], in_=tri[:], compare_op=ALU.is_ge, fill=0.0, base=0,
                                    pattern=[[1, P]], channel_multiplier=-1).then_inc(masks_made, 1)
            nc.gpsimd.affine_select(out=below[:], in_=below[:], compare_op=ALU.is_gt, fill=0.0, base=0,
                                    pattern=[[-1, P]], channel_multiplier=1).then_inc(masks_made, 1)
            pool.wait_ge(masks_made, 10)

            def wait_apart(s, value):
                pool.wait_ge(s, value)
                pool.sem_inc(sem("pool_waited"), 1)

            setup = Chain(pool, sem("pool_setup"), 0)
            setup.group(0)

            def prepare(step, f):
                for kind, t, what in in_order.get((step, f), []):
                    if kind in ("scale", "small"):
                        n = scale_order.index(t)
                        pool.wait_ge(sem("norm_ready"), n + 1)
                        setup(nc.gpsimd.partition_all_reduce(sc[:, t, 1:2], sc[:, t, 0:1], P, RMAX))
                        setup(nc.gpsimd.tensor_scalar(sc[:, t, 1:2], sc[:, t, 1:2], TINY,
                                                      BF_SLACK / TOP ** 2, ALU.max, ALU.mult))
                        nc.gpsimd.tensor_tensor(sc[:, t, 2:3], sc[:, t, 1:2], c_half[:, 0:1], ALU.pow)\
                            .then_inc(sem("raw_scale_ready"), 1)
                    if kind == "split":
                        for u in what:
                            if path[u] == "p":
                                pool.wait_ge(sem("hi_p"), rank[u] + 1)
                                nc.gpsimd.tensor_tensor(Wh[:, u, 1], scaled_p[:, rank[u] % 2], Wh[:, u, 0],
                                                        ALU.subtract).then_inc(split_p, 1)

            chain_a = Chain(pool, sem("pool_a"), 3, wait_apart)
            chain_c = Chain(pool, sem("pool_c"), 3, wait_apart)

            def inv_std(chain, dst, var, factor, shift, ready):
                chain(nc.gpsimd.tensor_scalar(dst, var, factor, shift, ALU.mult, ALU.add))
                nc.gpsimd.tensor_tensor(dst, dst, c_half[:, 0:TILES], ALU.pow).then_inc(ready, 1)

            def a_norm(g):
                wait_apart(sem("stats_a_ready"), g + 1)
                inv_std(chain_a, s_a[:, 1], mv_a[:, :, 1], 1.0 + EPS, EPS * EPS, sem("rstd2_a_ready"))
                inv_std(chain_a, s_a[:, 0], mv_a[:, :, 1], 1.0, EPS, sem("rstd_a_ready"))

            def a_scan_in(g):
                pool.wait_ge(sem("a_ready"), g + 1)
                for j in range(TILES):
                    if j == 0:
                        prev(g, 3, 3, pool, sem("dec_ps_ready"))
                    nc.gpsimd.tensor_tensor(ra[:, j], tri[:].unsqueeze(1).broadcast_to([P, H, P]),
                                            a_t[:, j].unsqueeze(2).broadcast_to([P, H, P]), ALU.mult)\
                        .then_inc(sem("ra_ready"), 1)

            def a_tdt(g):
                for j in range(TILES):
                    nc.gpsimd.tensor_tensor(tdt[:, j], tri[:].unsqueeze(1).broadcast_to([P, H, P]),
                                            dts[:, 4, j].unsqueeze(2).broadcast_to([P, H, P]), ALU.mult)\
                        .then_inc(sem("tdt_ready"), 1)

            def a_xd(g):
                prev(g, 2, 2, pool, sem("o_ps_ready"))
                wait_apart(sem("xbc_ready"), g * 3 + 1)
                for h in range(H):
                    nc.gpsimd.tensor_scalar(y[:, h], xbc[:, 0], rowt[:, 4 + h:5 + h], None, ALU.mult)\
                        .then_inc(sem("xd_ready"), 1)

            def a_xw(g):
                pool.wait_ge(sem("w0_ready"), g + 1)
                pool.wait_ge(sem("tok_ready"), g + 1)
                prev(g, 2, 2, pool, sem("y_ps_ready"))
                nc.gpsimd.tensor_tensor(xw[:], tok[:, 0].unsqueeze(1).broadcast_to([P, H, P]),
                                        w0[:].unsqueeze(2).broadcast_to([P, H, P]), ALU.mult)\
                    .then_inc(sem("xw_ready"), 1)

            def a_ce(g):
                pool.wait_ge(sem("exp_ready"), g * 3 + 3)
                nc.gpsimd.tensor_tensor(ce[:], ce[:], xbc[:, 2:6, P:SEQ], ALU.mult)\
                    .then_inc(sem("ce_ready"), 1)

            def a_rms(g):
                wait_apart(sem("sumsq_ready"), g * 2 + 2)
                inv_std(chain_a, ss[:, 1], ss[:, 0], 1.0 / D, EPS, sem("rms_ready"))

            def b_copy(g):
                if not (isinstance(g, int) and g == 0):
                    wait_apart(sem("mlp_ready"), g * 2)
                wait_apart(sem("h1_ready"), g * 2 + 2)
                nc.gpsimd.tensor_copy(h1b[:], h01[:]).then_inc(sem("h1b_ready"), 1)

            def norm_c(g, n, scale):
                wait_apart(sem("stats_c_ready"), g * 3 + n)
                inv_std(chain_c, s_c[:], mv_c[:, :, 1], 1.0 / scale ** 2, EPS / scale ** 2,
                        sem("rstd_c_ready"))

            def step(a, b, c):
                if a is not None:
                    chain_a.group(a)
                if c is not None:
                    chain_c.group(c)
                if a is not None:
                    a_norm(a)
                if isinstance(a, int) and a == 0:
                    prepare(0, 0)
                if c is not None:
                    norm_c(c, 1, 1.0)
                    norm_c(c, 2, ACT_SCALE)
                if b is not None:
                    b_copy(b)
                for f in range(1, 6) if isinstance(a, int) and a == 0 else []:
                    prepare(0, f)
                for f in range(FBLK) if isinstance(b, int) and b == 0 else []:
                    prepare(1, f)
                if a is not None:
                    a_xd(a)
                    a_scan_in(a)
                    a_tdt(a)
                for f in (6, 7, 8) if isinstance(a, int) and a == 0 else []:
                    prepare(0, f)
                if a is not None:
                    a_xw(a)
                    a_ce(a)
                for f in (9, 10, 11) if isinstance(a, int) and a == 0 else []:
                    prepare(0, f)
                if c is not None:
                    norm_c(c, 3, 1.0)
                if a is not None:
                    a_rms(a)
                    chain_a.close()
                for f in (12, 13) if isinstance(a, int) and a == 0 else []:
                    prepare(0, f)
                if c is not None:
                    chain_c.close()

            steps(pool, step)

        @block.scalar
        def _(eng):
            chain_a = Chain(eng, sem("act_a"), 2)

            def prep_a():
                eng.wait_ge(small_loaded, 64)
                nc.scalar.activation(neg_a[:], rowt[:, 0:4], ACT.Exp).then_inc(sem("exp_a_log"), 1)

            scaling = Chain(eng, sem("act_scaling"), 0)
            scaling.group(0)

            def prepare(step, f):
                for kind, t, what in in_order.get((step, f), []):
                    if kind == "small":
                        raw, w = (dt_raw, dt_w) if t == T_DT else (gl_raw, gl_w)
                        eng.wait_ge(sem("small_scaled"), 1 + (t == T_GL))
                        nc.scalar.activation(w[:, 0], raw[:], ACT.Copy).then_inc(sem("small_hi"), 1)
                    for u in what if kind == "split" else []:
                        n = rank[u]
                        if path[u] == "p":
                            eng.wait_ge(sem("scale_ready"), scale_order.index(t) + 1)
                            if n >= 2:
                                eng.wait_ge(split_p, n - 1)
                            scaling(nc.scalar.activation(scaled_p[:, n % 2], W[:, u], ACT.Copy,
                                                         scale=sc[:, t, 3:4]))
                            nc.scalar.activation(Wh[:, u, 0], scaled_p[:, n % 2], ACT.Copy)\
                                .then_inc(sem("hi_p"), 1)
                        else:
                            eng.wait_ge(sem("scaled_d_ready"), n + 1)
                            nc.scalar.activation(Wh[:, u, 0], scaled_d[:, n % 2], ACT.Copy)\
                                .then_inc(sem("hi_d"), 1)

            def a_t1(g):
                for b in range(2):
                    eng.wait_ge(sem("ht_ps_ready"), g * 2 + b + 1)
                    prev(g, 2, 2, eng, sem("z_ps_ready"))
                    nc.scalar.activation(ht[:, 0, 2 * b:2 * b + 2].rearrange("p k s -> p (k s)"),
                                         WA[b][:], ACT.Copy).then_inc(sem("ht_hi"), 1)

            XB_BANK = [2, 0, 1]

            def a_conv(g, b):
                eng.wait_ge(sem("xbc_ps_ready"), g * 3 + b + 1)
                src = WA[XB_BANK[b]]
                if b == 0:
                    prev(g, 3, 3, eng, sem("dec_ps_ready"))
                    prev(g, 2, 2, eng, sem("att_ps_ready"))
                    prev(g, 1, 1, eng, sem("ce_ready"))
                    prev(g, 4, 4, eng, sem("xd_ready"))
                for m in range(2):
                    c = 2 * b + m
                    nc.scalar.activation(xbc[:, c], src[:, m * SEQ:(m + 1) * SEQ], ACT.Identity,
                                         bias=conv_b[:, c:c + 1],
                                         scale=cw[:, c * TAPS + TAPS - 1:c * TAPS + TAPS])\
                        .then_inc(sem("tap_ready"), 1)
                nc.scalar.activation(pad[:, 2 * b:2 * b + 2, TAPS - 1:],
                                     src[:].rearrange("p (m s) -> p m s", m=2), ACT.Copy)\
                    .then_inc(sem("pad_ready"), 1)

            def a_silu(g, b):
                eng.wait_ge(sem("conv_ready"), g * XBC + 2 * b + 2)
                nc.scalar.activation(xbc[:, 2 * b:2 * b + 2], xbc[:, 2 * b:2 * b + 2], ACT.Silu)\
                    .then_inc(sem("xbc_ready"), 1)

            def a_z(g, b):
                eng.wait_ge(sem("z_ps_ready"), g * 2 + b + 1)
                prev(g, 2, 2, eng, sem("y_ready"))
                nc.scalar.activation(sz[:, 2 * b:2 * b + 2], WA[b][:].rearrange("p (m s) -> p m s", m=2),
                                     ACT.Silu, scale=inv_in).then_inc(sem("sz_ready"), 1)

            def a_dt(g):
                eng.wait_ge(sem("dtv_ready"), g + 1)
                chain_a(nc.scalar.activation(dts[:, 1], dts[:, 0], ACT.Abs))
                chain_a(nc.scalar.activation(dts[:, 2], dts[:, 1], ACT.Exp, scale=-1.0))
                nc.scalar.activation(dts[:, 3], dts[:, 2], ACT.Ln, bias=1.0).then_inc(sem("log_ready"), 1)

            def a_tok(g):
                eng.wait_ge(sem("tok_ps_ready"), g + 1)
                prev(g, 2, 2, eng, sem("y_ps_ready"))
                nc.scalar.activation(tok[:].rearrange("p m s -> p (m s)"), WA[2][:, 0:3 * P], ACT.Copy)\
                    .then_inc(sem("tok_ready"), 1)

            def a_exp(g, n):
                eng.wait_ge(sem("dec_ps_ready"), g * 3 + n + 1)
                if n == 0:
                    prev(g, 2, 2, eng, sem("y_ps_ready"))
                if n == 2:
                    eng.wait_ge(sem("decdt_ready"), g * 2 + 2)
                dst = dec[:, n] if n < TILES else ce[:]
                nc.scalar.activation(dst.rearrange("p h q -> p (h q)"), WA[[0, 1, 0][n]][:], ACT.Exp)\
                    .then_inc(sem("exp_ready"), 1)

            def a_state(g):
                eng.wait_ge(sem("st_ps_ready"), g + 1)
                nc.scalar.activation(xw[:].rearrange("p h q -> p (h q)"), WA[2][:], ACT.Copy)\
                    .then_inc(sem("state_ready"), 1)

            def a_sumsq(g, j):
                eng.wait_ge(sem("h1_ready"), g * 2 + j + 1)
                if j == 0:
                    prev(g, 2, 2, eng, sem("h2t_ps_ready"))
                nc.scalar.activation(hn[:, j], h01[:, j], ACT.Square, accum_out=ss[:, 0, j:j + 1])\
                    .then_inc(sem("sumsq_ready"), 1)

            def a_t2(g):
                for b in range(2):
                    eng.wait_ge(sem("h2t_ps_ready"), g * 2 + b + 1)
                    prev(g, FBLK, FBLK, eng, sem("gu_ready"))
                    nc.scalar.activation(h2t[:, 0, 2 * b:2 * b + 2].rearrange("p k s -> p (k s)"),
                                         WA[1 + b][:], ACT.Copy).then_inc(sem("h2t_hi"), 1)

            def b_silu(g, f):
                eng.wait_ge(sem("gu_ready"), g * FBLK + f + 1)
                if f >= 2:
                    eng.wait_ge(sem("act_ready"), g * FBLK + f - 1)
                else:
                    prev(g, FBLK, FBLK - 1 + f, eng, sem("act_ready"))
                nc.scalar.activation(sg[:, f % 2], GU[f % 2][:, 0:SEQ], ACT.Silu, scale=inv_gate)\
                    .then_inc(sem("sg_ready"), 1)

            def b_hi(g, f):
                eng.wait_ge(sem("prod_ready"), g * FBLK + f + 1)
                if f >= 4:
                    eng.wait_ge(sem("down_done"), g * FBLK + f - 3)
                else:
                    prev(g, FBLK, last_in_slot(f) + 1, eng, sem("down_done"))
                nc.scalar.activation(act[:, slot(f), 0], sg[:, f % 2], ACT.Copy)\
                    .then_inc(sem("act_hi"), 1)

            def c_t3(g, b):
                eng.wait_ge(sem("h3t_ps_ready"), g * 2 + b + 1)
                prev(g, 2, 2, eng, sem("u_ps_ready"))
                nc.scalar.activation(h3t[:, 0, 2 * b:2 * b + 2].rearrange("p k s -> p (k s)"), WC[:],
                                     ACT.Copy).then_inc(sem("h3t_hi"), 1)

            def c_zt(g):
                eng.wait_ge(sem("zt_ps_ready"), g + 1)
                nc.scalar.activation(zt[:], WC[0:E * R, 0:SEQ], ACT.Copy).then_inc(sem("zt_ready"), 1)

            def c_u(g, j):
                eng.wait_ge(sem("u_ps_ready"), g * 2 + j + 1)
                nc.scalar.activation(h3[:, j], WC[:], ACT.Copy, scale=inv_lin).then_inc(sem("u_ready"), 1)

            A_AT = {1: lambda g: a_t1(g), 2: lambda g: a_conv(g, 0),
                    3: lambda g: (a_conv(g, 1), a_conv(g, 2), a_silu(g, 0)),
                    4: lambda g: (a_silu(g, 1), a_z(g, 0), a_dt(g)),
                    5: lambda g: (a_silu(g, 2), a_z(g, 1), a_tok(g)),
                    6: lambda g: (a_exp(g, 0), a_exp(g, 1)), 8: lambda g: (a_exp(g, 2), a_state(g)),
                    10: lambda g: a_sumsq(g, 0), 11: lambda g: a_sumsq(g, 1), 13: lambda g: a_t2(g)}
            C_AT = {4: lambda g: c_t3(g, 0), 5: lambda g: c_t3(g, 1), 7: lambda g: c_zt(g),
                    8: lambda g: c_u(g, 0), 9: lambda g: c_u(g, 1)}

            def step(a, b, c):
                if a is not None:
                    chain_a.group(a)
                if isinstance(a, int) and a == 0:
                    prep_a()
                for f in range(FBLK):
                    if isinstance(a, int) and a <= 1:
                        prepare(a, f)
                    if b is not None:
                        b_silu(b, f)
                        b_hi(b, f)
                    if a is not None and f in A_AT:
                        A_AT[f](a)
                    if c is not None and f in C_AT:
                        C_AT[f](c)
                if a is not None:
                    chain_a.close()

            steps(eng, step)

        @block.vector
        def _(dve):
            setup = Chain(dve, sem("dve_setup"), 0)
            setup.group(0)

            def wait_apart(s, value):
                dve.wait_ge(s, value)
                dve.sem_inc(sem("dve_waited"), 1)

            chain_a = Chain(dve, sem("dve_a"), 20, wait_apart)
            chain_c = Chain(dve, sem("dve_c"), 15, wait_apart)

            def scale_done(t, products):
                s = sc[:, t]
                dve.wait_ge(sem("raw_scale_ready"), scale_order.index(t) + 1)
                nc.vector.tensor_single_scalar(s[:, 3:4].bitcast(I32), s[:, 2:3].bitcast(I32), POW2,
                                               ALU.bitwise_and).then_inc(sem("scale_ready"), 1)
                dve.wait_ge(sem("scale_ready"), scale_order.index(t) + 1)
                setup(nc.vector.reciprocal(s[:, 4:5], s[:, 3:4]))
                setup(nc.vector.tensor_scalar(s[:, 4:5], s[:, 4:5], products, None, ALU.mult))

            def ln_rows():
                for n in range(2):
                    m, r = bound[:, 6 + n:7 + n], bound[:, 8 + n:9 + n]
                    setup(nc.vector.tensor_reduce(m, lnt[:, n], AX.X, ALU.max, apply_absolute_value=True))
                    setup(nc.vector.tensor_scalar(m, m, TINY, ROOT_D / TOP, ALU.max, ALU.mult))
                    setup(nc.vector.reciprocal(r, m))
                    setup(nc.vector.tensor_single_scalar(ln_scale[:, n:n + 1].bitcast(I32), r.bitcast(I32), POW2,
                                                         ALU.bitwise_and))
                    setup(nc.vector.reciprocal(m, ln_scale[:, n:n + 1]))
                    setup(nc.vector.tensor_scalar(lnt[:, n], lnt[:, n], ln_scale[:, n:n + 1], None, ALU.mult))

            inv_ln = [bound[:, 6:7], bound[:, 7:8]]

            def prep_norms(n):
                a, b = PIECES[n]
                dve.wait_ge(sem("gram_ready"), piece_order.index(n) + 1)
                for u in range(a, b):
                    ins = nc.vector.tensor_tensor_reduce(
                        out=square[:, (u - a) * P:(u - a + 1) * P], in0=WC[:, (u - a) * P:(u - a + 1) * P],
                        in1=ident[:], scale=1.0, scalar=0.0, op0=ALU.mult, op1=ALU.add,
                        accum_out=norms[:, u:u + 1])
                    if u == b - 1:
                        ins.then_inc(sem("gram_read"), 1)
                dve.wait_ge(sem("gram_read"), piece_order.index(n) + 1)

            def prep_scale(t):
                us = UNITS_OF[t]
                nc.vector.tensor_reduce(sc[:, t, 0:1], norms[:, us[0]:us[-1] + 1], AX.X, ALU.max)\
                    .then_inc(sem("norm_ready"), 1)
                scale_done(t, {T_IN: inv_ln[0], T_GATE: inv_ln[1], T_UP: inv_ln[1], T_DOWN: 1.0,
                               T_LIN: 1.0 / ACT_SCALE}[t])
                if t == T_IN:
                    setup(nc.vector.tensor_scalar(cw[:], conv_w, inv_in, None, ALU.mult))
                    dve.wait_ge(sem("exp_a_log"), 1)
                    setup(nc.vector.tensor_scalar(neg_a[:], neg_a[:], -1.0, None, ALU.mult))
                if t == T_UP:
                    setup(nc.vector.tensor_scalar(act_scale, inv_gate, inv_up, 2.0 ** 45, ALU.mult, ALU.mult))
                    setup(nc.vector.reciprocal(act_scale, act_scale))
                    setup(nc.vector.tensor_scalar(up_to_act, act_scale, inv_up, None, ALU.mult))
                if t == T_DOWN:
                    setup(nc.vector.reciprocal(inv_down, act_scale))
                    setup(nc.vector.tensor_scalar(inv_down, inv_down, sc[:, t, 4:5], None, ALU.mult))

            def prep_small(t):
                raw, w, n = (dt_raw, dt_w, 0) if t == T_DT else (gl_raw, gl_w, 1)
                dve.wait_ge(*((small_loaded, 64) if t == T_DT else (lora_loaded, 32)))
                setup(nc.vector.tensor_reduce(mabs[:, n], raw[:], AX.X, ALU.max, apply_absolute_value=True))
                setup(nc.vector.tensor_tensor(mabs[:, n], mabs[:, n], mabs[:, n], ALU.mult))
                nc.vector.tensor_reduce(sc[:, t, 0:1], mabs[:, n], AX.X, ALU.max).then_inc(sem("norm_ready"), 1)
                scale_done(t, inv_ln[0] if t == T_DT else 1.0 / ACT_SCALE)
                nc.vector.tensor_scalar(raw[:], raw[:], sc[:, t, 3:4], None, ALU.mult)\
                    .then_inc(sem("small_scaled"), 1)
                if t == T_GL:
                    setup(nc.vector.tensor_scalar(lora_scale, inv_gl, sc[:, T_LIN, 3:4], ACT_SCALE,
                                                  ALU.mult, ALU.mult))
                dve.wait_ge(sem("small_hi"), 1 + n)
                nc.vector.tensor_tensor(w[:, 1], raw[:], w[:, 0], ALU.subtract).then_inc(small_split, 1)

            def prep_split(t, units):
                units = [u for u in units if path[u] == "d"]

                def lo(u):
                    n = rank[u]
                    dve.wait_ge(sem("hi_d"), n + 1)
                    nc.vector.tensor_tensor(Wh[:, u, 1], scaled_d[:, n % 2], Wh[:, u, 0], ALU.subtract)\
                        .then_inc(split_d, 1)

                for m, u in enumerate(units):
                    n = rank[u]
                    if n >= 2:
                        dve.wait_ge(split_d, n - 1)
                    nc.vector.tensor_scalar(scaled_d[:, n % 2], W[:, u], sc[:, t, 3:4], None, ALU.mult)\
                        .then_inc(sem("scaled_d_ready"), 1)
                    if m:
                        lo(units[m - 1])
                lo(units[-1])

            def prepare(step, f):
                for kind, t, what in in_order.get((step, f), []):
                    {"norms": lambda: prep_norms(what), "scale": lambda: prep_scale(t),
                     "small": lambda: prep_small(t), "split": lambda: prep_split(t, what)}[kind]()

            def stats(chain, src, st, mv, done):
                for j in range(TILES):
                    chain(nc.vector.bn_stats(st[:, j], src[:, j]), wait=j == TILES - 1)
                chain(nc.vector.bn_aggr(mv[:, 0], st[:, 0]), wait=False)
                nc.vector.bn_aggr(mv[:, 1], st[:, 1]).then_inc(done, 1)

            def a_stats(g):
                dve.wait_ge(x_loaded, g * 16 + 16)
                prev(g, 1, 1, dve, sem("rstd_a_ready"))
                stats(chain_a, xa, stats_a, mv_a, sem("stats_a_ready"))

            def a_center(g):
                prev(g, 2, 2, dve, sem("h2t_ps_ready"))
                dve.wait_ge(sem("stats_a_ready"), g + 1)
                for j in range(TILES):
                    nc.vector.scalar_tensor_tensor(hn[:, j], xa[:, j], mv_a[:, j, 0:1], lnt[:, 0],
                                                   ALU.subtract, ALU.mult).then_inc(sem("centered"), 1)

            def a_norm(g):
                dve.wait_ge(sem("rstd2_a_ready"), g + 1)
                for j in range(TILES):
                    dve.wait_ge(sem("centered"), g * 2 + j + 1)
                    nc.vector.tensor_scalar(hn[:, j], hn[:, j], s_a[:, 1, j:j + 1], None, ALU.mult)\
                        .then_inc(sem("hn_ready"), 1)

            def a_h0(g):
                dve.wait_ge(sem("rstd_a_ready"), g + 1)
                prev(g, 1, 1, dve, sem("h1b_ready"))
                for j in range(TILES):
                    nc.vector.tensor_scalar(h01[:, j], xa[:, j], mv_a[:, j, 0:1], s_a[:, 0, j:j + 1],
                                            ALU.subtract, ALU.mult).then_inc(sem("h0_ready"), 1)

            def a_t1(g):
                for b in range(2):
                    dve.wait_ge(sem("ht_hi"), g * 2 + b + 1)
                    nc.vector.tensor_tensor(ht[:, 1, 2 * b:2 * b + 2].rearrange("p k s -> p (k s)"), WA[b][:],
                                            ht[:, 0, 2 * b:2 * b + 2].rearrange("p k s -> p (k s)"),
                                            ALU.subtract).then_inc(sem("ht_ready"), 1)

            def a_conv(g, b):
                dve.wait_ge(sem("pad_ready"), g * 3 + b + 1)
                for k in range(TAPS - 1):
                    for m in range(2):
                        c = 2 * b + m
                        ins = nc.vector.scalar_tensor_tensor(
                            xbc[:, c], pad[:, c, k:k + SEQ], cw[:, c * TAPS + k:c * TAPS + k + 1],
                            xbc[:, c], ALU.mult, ALU.add)
                        if k == TAPS - 2:
                            ins.then_inc(sem("conv_ready"), 1)
                        elif m == 1:
                            chain_a(ins)
                        else:
                            ins.then_inc(sem("conv_part"), 1)
                    if k < TAPS - 2:
                        dve.wait_ge(sem("conv_part"), g * 6 + b * 2 + k + 1)

            def a_dtv(g):
                dve.wait_ge(sem("dt_ps_ready"), g + 1)
                nc.vector.scalar_tensor_tensor(
                    dts[:, 0], WA[2][:, 0:TILES * H].rearrange("p (t h) -> p t h", h=H), inv_dt,
                    rowt[:, 8:12].unsqueeze(1).broadcast_to([P, TILES, H]), ALU.mult, ALU.add)\
                    .then_inc(sem("dtv_ready"), 1)

            def a_dt(g):
                dve.wait_ge(sem("log_ready"), g + 1)
                v, e, log, t, s = dts[:, 0], dts[:, 2], dts[:, 3], dts[:, 1], dts[:, 5]
                chain_a(nc.vector.tensor_scalar(t, e, 0.2, -0.25, ALU.mult, ALU.add))
                for c in (0.0, 1.0 / 3, -0.5, 1.0):
                    if c:
                        chain_a(nc.vector.scalar_tensor_tensor(t, t, c, e, ALU.add, ALU.mult))
                    else:
                        chain_a(nc.vector.tensor_tensor(t, t, e, ALU.mult))
                chain_a(nc.vector.tensor_tensor(t, t, log, ALU.subtract))
                chain_a(nc.vector.scalar_tensor_tensor(s, e, SERIES, t, ALU.is_lt, ALU.mult))
                chain_a(nc.vector.tensor_tensor(s, s, log, ALU.add))
                chain_a(nc.vector.scalar_tensor_tensor(dts[:, 4], v, 0.0, s, ALU.max, ALU.add))
                nc.vector.tensor_tensor(a_t[:], dts[:, 4], neg_a[:].unsqueeze(1).broadcast_to([P, TILES, H]),
                                        ALU.mult).then_inc(sem("a_ready"), 1)

            def flat(t):
                return t.rearrange("p h q -> p (h q)")

            def a_dec(g, j):
                dve.wait_ge(sem("exp_ready"), g * 3 + j + 1)
                dve.wait_ge(sem("tdt_ready"), g * 2 + j + 1)
                nc.vector.tensor_tensor(flat(dec[:, j]), flat(dec[:, j]), flat(tdt[:, j]), ALU.mult)\
                    .then_inc(sem("decdt_ready"), 1)
                dve.wait_ge(sem("decdt_ready"), g * 2 + j + 1)
                if j == 0:
                    nc.vector.tensor_copy(w0[:], dec[:, 0, :, P - 1]).then_inc(sem("w0_ready"), 1)
                    dve.wait_ge(sem("w0_ready"), g + 1)

            def a_att(g, j):
                dve.wait_ge(sem("att_ps_ready"), g * 2 + j + 1)
                nc.vector.tensor_tensor(flat(dec[:, j]), flat(dec[:, j]), WA[[2, 1][j]][:], ALU.mult)\
                    .then_inc(sem("attw_ready"), 1)

            def a_y(g, j):
                dve.wait_ge(sem("y_ps_ready"), g * 2 + j + 1)
                dve.wait_ge(sem("xd_ready"), g * 4 + 4)
                dve.wait_ge(sem("sz_ready"), g * 2 + 2)
                q = slice(j * P, j * P + P)
                chain_a(nc.vector.tensor_tensor(y[:, :, q], WA[j][:].rearrange("p (h q) -> p h q", h=H),
                                                y[:, :, q], ALU.add))
                nc.vector.tensor_tensor(y[:, :, q], y[:, :, q], sz[:, :, q], ALU.mult)\
                    .then_inc(sem("y_ready"), 1)

            def a_h1(g, j):
                dve.wait_ge(sem("o_ps_ready"), g * 2 + j + 1)
                nc.vector.tensor_tensor(h01[:, j], WA[[2, 0][j]][:], h01[:, j], ALU.add)\
                    .then_inc(sem("h1_ready"), 1)

            def a_h2(g, j):
                dve.wait_ge(sem("rms_ready"), g + 1)
                nc.vector.scalar_tensor_tensor(hn[:, j], h01[:, j], ss[:, 1, j:j + 1], lnt[:, 1],
                                               ALU.mult, ALU.mult).then_inc(sem("h2_ready"), 1)

            def a_t2(g):
                for b in range(2):
                    dve.wait_ge(sem("h2t_hi"), g * 2 + b + 1)
                    nc.vector.tensor_tensor(h2t[:, 1, 2 * b:2 * b + 2].rearrange("p k s -> p (k s)"), WA[1 + b][:],
                                            h2t[:, 0, 2 * b:2 * b + 2].rearrange("p k s -> p (k s)"),
                                            ALU.subtract).then_inc(sem("h2t_ready"), 1)

            def b_prod(g, f):
                dve.wait_ge(sem("sg_ready"), g * FBLK + f + 1)
                nc.vector.scalar_tensor_tensor(sg[:, f % 2], GU[f % 2][:, SEQ:2 * SEQ], up_to_act, sg[:, f % 2],
                                               ALU.mult, ALU.mult).then_inc(sem("prod_ready"), 1)

            def b_lo(g, f):
                dve.wait_ge(sem("act_hi"), g * FBLK + f + 1)
                nc.vector.tensor_tensor(act[:, slot(f), 1], sg[:, f % 2], act[:, slot(f), 0], ALU.subtract)\
                    .then_inc(sem("act_ready"), 1)

            def b_mlp(g):
                dve.wait_ge(sem("h1b_ready"), g + 1)
                for j in range(TILES):
                    if j == 0:
                        dve.wait_ge(sem("acc0_ready"), g + 1)
                    else:
                        dve.wait_ge(sem("down_done"), g * FBLK + FBLK)
                    nc.vector.scalar_tensor_tensor(mlp[:, j], ACC[j][:], inv_down, h1b[:, j], ALU.mult, ALU.add)\
                        .then_inc(sem("mlp_ready"), 1)

            def c_stats1(g):
                dve.wait_ge(sem("mlp_ready"), g * 2 + 2)
                prev(g, 3, 3, dve, sem("rstd_c_ready"))
                stats(chain_c, mlp, stats_c, mv_c, sem("stats_c_ready"))

            def c_norm(g, n, src, dst, ready):
                dve.wait_ge(sem("rstd_c_ready"), g * 3 + n)
                for j in range(TILES):
                    nc.vector.tensor_scalar(dst[:, j], src[:, j], mv_c[:, j, 0:1], s_c[:, j:j + 1],
                                            ALU.subtract, ALU.mult).then_inc(ready, 1)

            def c_x1(g):
                prev(g, 16, 16, dve, stored)
                c_norm(g, 1, mlp, h3, sem("n1_ready"))
                dve.wait_ge(xc_loaded, g * 16 + 16)
                for j in range(TILES):
                    dve.wait_ge(sem("n1_ready"), g * 2 + j + 1)
                    nc.vector.tensor_tensor(x1[:, j], x1[:, j], h3[:, j], ALU.add).then_inc(sem("x1_ready"), 1)

            def c_stats2(g):
                dve.wait_ge(sem("x1_ready"), g * 2 + 2)
                stats(chain_c, x1, stats_c, mv_c, sem("stats_c_ready"))

            def c_h3(g):
                c_norm(g, 2, x1, h3, sem("h3_ready"))

            def c_t3(g, b):
                dve.wait_ge(sem("h3t_hi"), g * 2 + b + 1)
                nc.vector.tensor_tensor(h3t[:, 1, 2 * b:2 * b + 2].rearrange("p k s -> p (k s)"), WC[:],
                                        h3t[:, 0, 2 * b:2 * b + 2].rearrange("p k s -> p (k s)"),
                                        ALU.subtract).then_inc(sem("h3t_ready"), 1)

            def c_route(g):
                dve.wait_ge(sem("lg_ps_ready"), g + 1)
                src = WC[:, 0:TILES * (E + E * R)].rearrange("p (t n) -> p t n", t=TILES)
                chain_c(nc.vector.scalar_tensor_tensor(
                    lg[:], src[:, :, 0:E], inv_gl, rowt[:, 12:16].unsqueeze(1).broadcast_to([P, TILES, E]),
                    ALU.mult, ALU.add))
                nc.vector.tensor_scalar(zs[:], src[:, :, E:], lora_scale, None, ALU.mult)\
                    .then_inc(sem("zs_ready"), 1)
                chain_c(nc.vector.tensor_reduce(mx[:], lg[:], AX.X, ALU.max))
                chain_c(nc.vector.tensor_tensor(eq[:], lg[:], mx[:].unsqueeze(2).broadcast_to([P, TILES, E]),
                                                ALU.is_equal))
                chain_c(nc.vector.tensor_copy(seen[:, :, 0:1], eq[:, :, 0:1]))
                for e in range(1, E):
                    ins = nc.vector.tensor_tensor(seen[:, :, e:e + 1], seen[:, :, e - 1:e], eq[:, :, e:e + 1], ALU.max)
                    if e < E - 1:
                        chain_c(ins)
                    else:
                        ins.then_inc(sem("seen_ready"), 1)
                dve.wait_ge(sem("seen_ready"), g + 1)
                nc.vector.tensor_copy(hot[:, :, 0:1], seen[:, :, 0:1]).then_inc(sem("hot_part"), 1)
                nc.vector.tensor_tensor(hot[:, :, 1:E], seen[:, :, 1:E], seen[:, :, 0:E - 1], ALU.subtract)\
                    .then_inc(sem("hot_part"), 1)
                dve.wait_ge(sem("hot_part"), g * 2 + 2)
                dve.wait_ge(sem("zs_ready"), g + 1)
                zv = zs[:].rearrange("p t (e r) -> p (t e) r", r=R)
                hv = hot[:].rearrange("p t e -> p (t e)").unsqueeze(2).broadcast_to([P, TILES * E, R])
                nc.vector.tensor_tensor(zv, zv, hv, ALU.mult).then_inc(sem("zm_ready"), 1)

            def c_stats3(g):
                dve.wait_ge(sem("u_ready"), g * 2 + 2)
                stats(chain_c, h3, stats_c, mv_c, sem("stats_c_ready"))

            def c_out(g):
                c_norm(g, 3, h3, h3, sem("n3_ready"))
                for j in range(TILES):
                    dve.wait_ge(sem("n3_ready"), g * 2 + j + 1)
                    nc.vector.tensor_tensor(h3[:, j], h3[:, j], x1[:, j], ALU.add).then_inc(sem("out_ready"), 1)

            A_AT = {1: lambda g: a_t1(g), 2: lambda g: a_conv(g, 0), 3: lambda g: (a_conv(g, 1), a_dtv(g)),
                    4: lambda g: a_conv(g, 2), 5: lambda g: (a_dt(g), a_h0(g)),
                    7: lambda g: (a_dec(g, 0), a_dec(g, 1), a_att(g, 0)), 8: lambda g: a_att(g, 1),
                    9: lambda g: (a_y(g, 0), a_y(g, 1)), 10: lambda g: a_h1(g, 0), 11: lambda g: a_h1(g, 1),
                    12: lambda g: (a_h2(g, 0), a_h2(g, 1))}
            C_AT = {1: lambda g: c_x1(g), 2: lambda g: c_stats2(g), 3: lambda g: c_h3(g), 4: lambda g: c_t3(g, 0),
                    5: lambda g: c_t3(g, 1), 6: lambda g: c_route(g), 9: lambda g: c_stats3(g),
                    10: lambda g: c_out(g)}

            def step(a, b, c):
                if isinstance(a, int) and a == 0:
                    dve.wait_ge(masks_made, 10)
                    chain_a.group(0)
                    a_stats(0)
                    dve.wait_ge(small_loaded, 64)
                    ln_rows()
                    a_center(0)
                    dve.wait_ge(sem("stats_a_ready"), 1)
                    a_norm(0)
                if c is not None:
                    chain_c.group(c)
                if a is not None and not (isinstance(a, int) and a == 0):
                    chain_a.group(a)
                    a_stats(a)
                    a_center(a)
                for f in range(FBLK):
                    if isinstance(a, int) and a <= 1:
                        prepare(a, f)
                    if b is not None:
                        b_prod(b, f)
                        b_lo(b, f)
                    if f == 0:
                        if a is not None and not (isinstance(a, int) and a == 0):
                            a_norm(a)
                        if c is not None:
                            c_stats1(c)
                    if a is not None and f in A_AT:
                        A_AT[f](a)
                    if c is not None and f in C_AT:
                        C_AT[f](c)
                if a is not None:
                    a_t2(a)
                    chain_a.close()
                if b is not None:
                    b_mlp(b)
                if c is not None:
                    chain_c.close()

            steps(dve, step)

        @block.tensor
        def _(pe):
            def mm(dst, left, right, start, stop):
                return nc.tensor.matmul(dst, left, right, start=start, stop=stop)

            PAIRS = [(0, 0), (0, 1), (1, 0)]

            def split_product(dst, lefts, rights, start=True, stop=True):
                todo = [(lf[a], rt[b]) for lf, rt in zip(lefts, rights) for a, b in PAIRS]
                for n, (lf, rt) in enumerate(todo):
                    last = mm(dst, lf, rt, start and n == 0, stop and n == len(todo) - 1)
                return last

            def weight(u, k):
                return [Wh[:, u, s, k * P:(k + 1) * P] for s in range(2)]

            def tokens(t, k, j=None):
                q = slice(0, SEQ) if j is None else slice(j * P, j * P + P)
                return [t[:, s, k, q] for s in range(2)]

            def transposed(src, bank, b, ready):
                for k in range(2):
                    for j in range(TILES):
                        last = nc.tensor.transpose(bank[:, k * SEQ + j * P:k * SEQ + (j + 1) * P],
                                                   src[:, j, (2 * b + k) * P:(2 * b + k + 1) * P], ident[:])
                last.then_inc(ready, 1)

            def prepare(step, f):
                for kind, t, n in in_order.get((step, f), []):
                    if kind != "norms":
                        continue
                    a, b = PIECES[n]
                    pe.wait_ge(s_piece[n], 16)
                    if piece_order.index(n):
                        pe.wait_ge(sem("gram_read"), piece_order.index(n))
                    for u in range(a, b):
                        upper = W[:, u].bitcast(BF16).rearrange("p (n two) -> p n two", two=2)[:, :, 1]
                        for k in range(KB):
                            v = upper[:, k * P:(k + 1) * P]
                            last = mm(WC[:, (u - a) * P:(u - a + 1) * P], v, v, k == 0, k == KB - 1)
                    last.then_inc(sem("gram_ready"), 1)

            def a_t1(g):
                pe.wait_ge(sem("hn_ready"), g * 2 + 2)
                for b in range(2):
                    if b == 0:
                        prev(g, 2, 2, pe, sem("h1_ready"))
                    prev(g, 2, 1, pe, sem("h2t_ready"))
                    transposed(hn, WA[b], b, sem("ht_ps_ready"))

            def channels(g, units, bank, ready):
                for m, u in enumerate(units):
                    if isinstance(g, int) and g == 0:
                        wait_split(pe, [u])
                    last = split_product(bank[:, m * SEQ:(m + 1) * SEQ], [weight(u, k) for k in range(KB)],
                                         [tokens(ht, k) for k in range(KB)])
                last.then_inc(ready, 1)

            def a_in(g, b):
                pe.wait_ge(sem("ht_ready"), g * 2 + 2)
                if b == 0:
                    prev(g, 2, 2, pe, sem("h2t_ready"))
                channels(g, (2 * b, 2 * b + 1), WA[[2, 0, 1][b]], sem("xbc_ps_ready"))

            def a_dt(g):
                pe.wait_ge(sem("pad_ready"), g * 3 + 1)
                if isinstance(g, int) and g == 0:
                    pe.wait_ge(small_split, 1)
                for j in range(TILES):
                    last = split_product(WA[2][:, j * H:(j + 1) * H], [tokens(ht, k, j) for k in range(KB)],
                                         [[dt_w[:, s, k] for s in range(2)] for k in range(KB)])
                last.then_inc(sem("dt_ps_ready"), 1)

            def a_z(g, b):
                pe.wait_ge(sem("pad_ready"), g * 3 + 2 + b)
                channels(g, (6 + 2 * b, 7 + 2 * b), WA[b], sem("z_ps_ready"))

            def a_tok(g):
                pe.wait_ge(sem("xbc_ready"), g * 3 + 1)
                pe.wait_ge(sem("dtv_ready"), g + 1)
                for n, (c, j) in enumerate([(0, 0), (0, 1), (1, 0)]):
                    last = nc.tensor.transpose(WA[2][:, n * P:(n + 1) * P], xbc[:, c, j * P:(j + 1) * P], ident[:])
                last.then_inc(sem("tok_ps_ready"), 1)

            def flat(t):
                return t.rearrange("p h q -> p (h q)")

            def a_dec(g, n):
                if n < TILES:
                    pe.wait_ge(sem("sz_ready"), g * 2 + n + 1)
                    pe.wait_ge(sem("ra_ready"), g * 2 + n + 1)
                else:
                    pe.wait_ge(sem("exp_ready"), g * 3 + 1)
                mm(WA[[0, 1, 0][n]][:], (below if n < TILES else ones)[:], flat(ra[:, min(n, 1)]), True, True)\
                    .then_inc(sem("dec_ps_ready"), 1)

            def a_att(g, j):
                if j == 0:
                    pe.wait_ge(sem("tok_ready"), g + 1)
                    pe.wait_ge(sem("xbc_ready"), g * 3 + 3)
                else:
                    pe.wait_ge(sem("exp_ready"), g * 3 + 2)
                q = slice(j * P, j * P + P)
                mm(WA[[2, 1][j]][:], xbc[:, 1, q], xbc[:, 2:6, q], True, True)\
                    .then_inc(sem("att_ps_ready"), 1)

            def a_state(g):
                pe.wait_ge(sem("attw_ready"), g * 2 + 1)
                pe.wait_ge(sem("xw_ready"), g + 1)
                mm(WA[2][:], tok[:, 2], flat(xw[:]), True, True).then_inc(sem("st_ps_ready"), 1)

            def a_y(g, j):
                if j == 0:
                    pe.wait_ge(sem("exp_ready"), g * 3 + 3)
                    mm(WA[0][:], tok[:, 0], flat(dec[:, 0]), True, True).then_inc(sem("y_ps_ready"), 1)
                else:
                    pe.wait_ge(sem("attw_ready"), g * 2 + 2)
                    pe.wait_ge(sem("state_ready"), g + 1)
                    pe.wait_ge(sem("ce_ready"), g + 1)
                    mm(WA[1][:], tok[:, 1], flat(dec[:, 1]), True, False)
                    for h in range(H):
                        last = mm(WA[1][:, h * P:(h + 1) * P], xw[:, h], ce[:, h], False, h == H - 1)
                    last.then_inc(sem("y_ps_ready"), 1)

            def a_o(g, j):
                pe.wait_ge(sem("y_ready"), g * 2 + j + 1)
                if j == 0:
                    pe.wait_ge(sem("state_ready"), g + 1)
                bank = WA[[2, 0][j]]
                for k in range(KB):
                    last = mm(bank[:], y[:, k, j * P:(j + 1) * P], W[:, U_OUT + k], k == 0, k == KB - 1)
                last.then_inc(sem("o_ps_ready"), 1)

            def a_t2(g):
                pe.wait_ge(sem("h2_ready"), g * 2 + 2)
                for b in range(2):
                    if b == 0:
                        pe.wait_ge(sem("y_ready"), g * 2 + 2)
                    transposed(hn, WA[1 + b], b, sem("h2t_ps_ready"))

            def b_gu(g, f):
                if f == 0:
                    pe.wait_ge(sem("h2t_ready"), g * 2 + 2)
                if f >= 2:
                    pe.wait_ge(sem("prod_ready"), g * FBLK + f - 1)
                else:
                    prev(g, FBLK, FBLK - 1 + f, pe, sem("prod_ready"))
                for m, base in enumerate((U_GATE, U_UP)):
                    if isinstance(g, int) and g == 0:
                        wait_split(pe, [base + f])
                    last = split_product(GU[f % 2][:, m * SEQ:(m + 1) * SEQ],
                                         [weight(base + f, k) for k in range(KB)],
                                         [tokens(h2t, k) for k in range(KB)])
                last.then_inc(sem("gu_ready"), 1)

            def b_down(g, f):
                if f == 0:
                    prev(g, 2, 2, pe, sem("mlp_ready"))
                pe.wait_ge(sem("act_ready"), g * FBLK + f + 1)
                if isinstance(g, int) and g == 0:
                    wait_split(pe, [U_DOWN + f])
                for j in range(TILES):
                    left = [act[:, slot(f), s, j * P:(j + 1) * P] for s in range(2)]
                    last = split_product(ACC[j][:], [left], [[Wh[:, U_DOWN + f, s] for s in range(2)]],
                                         start=f == 0, stop=f == FBLK - 1)
                    if f == FBLK - 1 and j == 0:
                        last.then_inc(sem("acc0_ready"), 1)
                last.then_inc(sem("down_done"), 1)

            def c_t3(g, b):
                if b == 0:
                    pe.wait_ge(sem("h3_ready"), g * 2 + 2)
                    prev(g, 2, 2, pe, sem("u_ready"))
                else:
                    pe.wait_ge(sem("h3t_ready"), g * 2 + 1)
                transposed(h3, WC, b, sem("h3t_ps_ready"))

            def c_logits(g):
                pe.wait_ge(sem("h3t_ready"), g * 2 + 2)
                n = E + E * R
                for j in range(TILES):
                    last = split_product(WC[:, j * n:(j + 1) * n], [tokens(h3t, k, j) for k in range(KB)],
                                         [[gl_w[:, s, k] for s in range(2)] for k in range(KB)])
                last.then_inc(sem("lg_ps_ready"), 1)

            def c_zt(g):
                pe.wait_ge(sem("zm_ready"), g + 1)
                for j in range(TILES):
                    last = nc.tensor.transpose(WC[0:E * R, j * P:(j + 1) * P], zs[:, j], ident[:])
                last.then_inc(sem("zt_ps_ready"), 1)

            def c_u(g, j):
                if j == 0:
                    pe.wait_ge(sem("zt_ready"), g + 1)
                else:
                    pe.wait_ge(sem("u_ready"), g * 2 + 1)
                split_product(WC[:], [tokens(h3t, k, j) for k in range(KB)],
                              [[Wh[:, U_LIN + k, s] for s in range(2)] for k in range(KB)], stop=False)
                mm(WC[:], zt[:, j * P:(j + 1) * P], lorab[:], False, True).then_inc(sem("u_ps_ready"), 1)

            A_AT = {1: lambda g: a_t1(g), 2: lambda g: a_in(g, 0), 3: lambda g: (a_in(g, 1), a_in(g, 2), a_dt(g)),
                    4: lambda g: a_z(g, 0), 5: lambda g: (a_z(g, 1), a_tok(g)),
                    6: lambda g: (a_dec(g, 0), a_dec(g, 1)), 7: lambda g: (a_att(g, 0), a_dec(g, 2)),
                    8: lambda g: (a_att(g, 1), a_state(g)), 9: lambda g: (a_y(g, 0), a_y(g, 1)),
                    10: lambda g: a_o(g, 0), 11: lambda g: a_o(g, 1), 13: lambda g: a_t2(g)}
            C_AT = {4: lambda g: c_t3(g, 0), 5: lambda g: c_t3(g, 1), 6: lambda g: c_logits(g),
                    7: lambda g: c_zt(g), 8: lambda g: c_u(g, 0), 9: lambda g: c_u(g, 1)}

            def step(a, b, c):
                if isinstance(a, int) and a == 0:
                    pe.wait_ge(masks_made, 10)
                for f in range(FBLK):
                    if isinstance(a, int) and a <= 1:
                        prepare(a, f)
                    if isinstance(a, int) and a == 0 and f == 10:
                        pe.wait_ge(s_piece[piece_of(U_OUT)], 16)
                    if isinstance(c, int) and c == 0 and f == 4:
                        wait_split(pe, UNITS_OF[T_LIN])
                        pe.wait_ge(small_split, 2)
                        pe.wait_ge(lora_loaded, 32)
                    if b is not None:
                        b_gu(b, f)
                        if f:
                            b_down(b, f - 1)
                    if a is not None and f in A_AT:
                        A_AT[f](a)
                    if c is not None and f in C_AT:
                        C_AT[f](c)
                if b is not None:
                    b_down(b, FBLK - 1)

            steps(pe, step)


RING = 4


def slot(f):
    return f % RING


def last_in_slot(f):
    return max(b for b in range(FBLK) if slot(b) == slot(f))


_OUT = (2048, 512)


def kernel(**inputs):
    import numpy as np
    import concourse.bacc as bacc
    from concourse.bass_utils import run_bass_kernel_spmd

    a = {n.replace("L0_", ""): np.asarray(v) for n, v in inputs.items()}

    def by_output(w, blocks):
        return w.reshape(blocks, P, KB, P).transpose(0, 3, 2, 1)

    w_in = a["attn_w_in"]
    z_rows, xbc_rows, dt_rows = np.split(w_in, [H * P, H * P + XBC * P])
    gl = np.concatenate([a["ffn_gate_w"], a["ffn_lora_A"].reshape(E * R, D)])
    arrays = {
        "x": a["attn_hidden_states"].reshape(-1, D),
        "w_in": by_output(np.concatenate([xbc_rows, z_rows]), XBC + H),
        "w_dt": dt_rows.T.reshape(KB, P, H).transpose(1, 0, 2),
        "w_out": a["attn_w_out"].T.reshape(KB, P, D),
        "w_gate": by_output(a["attn_gate_w"], FBLK),
        "w_up": by_output(a["attn_up_w"], FBLK),
        "w_down": a["attn_down_w"].T.reshape(FBLK, P, D),
        "w_lin": a["ffn_W_up"].T.reshape(KB, P, D),
        "w_gl": gl.T.reshape(KB, P, E + E * R).transpose(1, 0, 2),
        "lora_b": a["ffn_lora_B"].transpose(0, 2, 1).reshape(E * R, D),
        "cols": np.concatenate([a["attn_conv_w"].reshape(XBC, P, TAPS).transpose(1, 0, 2).reshape(P, -1),
                                a["attn_conv_b"].reshape(XBC, P).T], axis=1),
        "rows": np.concatenate([a["attn_A_log"], a["attn_D"], a["attn_dt_bias"],
                                a["ffn_expert_bias"]])[None, :],
        "ln_rows": np.concatenate([a["attn_ln1_w"], a["attn_ln2_w"]])[None, :],
    }
    arrays = {f"in_{n}": np.ascontiguousarray(v) for n, v in arrays.items()}
    nc = bacc.Bacc("TRN2", target_bir_lowering=False, num_devices=1)
    args = [nc.dram_tensor(n, v.shape, mybir.dt.from_np(v.dtype), kind="ExternalInput").ap()
            for n, v in arrays.items()]
    out = nc.dram_tensor("out_x", _OUT, F32, kind="ExternalOutput").ap()
    build(nc, *args, out)
    r = run_bass_kernel_spmd(nc, [arrays], core_ids=[0])
    return r.results[0]["out_x"].reshape(a["attn_hidden_states"].shape)
```

```python
from contextlib import ExitStack

import concourse.bass as bass
from concourse import mybir

F32 = mybir.dt.float32
F16 = mybir.dt.float16
BF16 = mybir.dt.bfloat16
I32 = mybir.dt.int32
ALU = mybir.AluOpType
ACT = mybir.ActivationFunctionType
AX = mybir.AxisListType
RMAX = bass.bass_isa.ReduceOp.max
RADD = bass.bass_isa.ReduceOp.add

P = 128
D = 512
KB = D // P
SEQ = 256
TILES = SEQ // P
GROUPS = 8
H = 4
TAPS = 4
FBLK = 14
XBC = 6
E = 4
R = 8
EPS = 1e-5

U_IN, U_OUT, U_GATE, U_UP, U_DOWN, U_LIN, UNITS = 0, 10, 14, 28, 42, 56, 60

ROOT_D = 22.63
ACT_SCALE = 64.0
TOP = 30000.0
BF_SLACK = 1.02
SERIES = 1.0 / 64
TINY = 1e-6
POW2 = 0x7F800000


class Chain:

    def __init__(self, eng, sem, per, wait=None):
        self.eng, self.sem, self.per, self.wait = eng, sem, per, wait or eng.wait_ge

    def group(self, g):
        self.g, self.k = g, 0

    def __call__(self, ins, wait=True):
        self.k += 1
        ins.then_inc(self.sem, 1)
        if wait:
            self.wait(self.sem, self.g * self.per + self.k)

    def close(self):
        assert self.k == self.per, (self.sem, self.k)


def build(nc, x, w_in, w_dt, w_out, w_gate, w_up, w_down, w_lin, w_gl, lora_b, cols, rows, ln_rows, out):
    x_g = x.rearrange("(g t p) d -> g p t d", t=TILES, p=P)
    out_g = out.rearrange("(g t p) d -> g t p d", t=TILES, p=P)
    ctx = ExitStack()
    with ctx:
        def sb(name, shape, dt=F32):
            return ctx.enter_context(nc.sbuf_tensor(name, shape, dt))

        def ps(name):
            return ctx.enter_context(nc.psum_tensor(name, [P, 512], F32))

        made = {}

        def sem(name):
            if name not in made:
                made[name] = ctx.enter_context(nc.semaphore(name))
            return made[name]

        W = sb("weights", [P, UNITS, 512])
        Wh = W[:].bitcast(F16).rearrange("p u (s n) -> p u s n", s=2)
        dt_raw = sb("dt_raw", [P, KB, H])[:]
        dt_w = sb("dt_w", [P, 2, KB, H], F16)
        gl_w = sb("gl_w", [P, 2, KB, E + E * R], F16)
        lora_1 = sb("lora_b_1", [4 * E * R, D], BF16)
        lora_2 = sb("lora_b_2", [2 * E * R, D], BF16)
        colt = sb("cols_t", [P, 30])
        conv_w, conv_b = colt[:, 0:24], colt[:, 24:30]
        lnt = sb("ln_rows_t", [P, 2, D])
        rowt = sb("rows_t", [P, 16])
        neg_a = sb("neg_a", [P, H])
        cw = sb("conv_ws", [P, XBC * TAPS])
        ident = sb("ident", [P, P])
        tri = sb("tri", [P, P])
        below = sb("below", [P, P])
        ones = sb("ones", [P, P])
        sc = sb("scales", [P, 7, 5])
        bound = sb("bound", [P, 10])
        minus_half = sb("minus_half", [P, TILES])

        xa = sb("xa", [P, TILES, D])
        h01 = sb("h01", [P, TILES, D])
        hn = sb("hn", [P, TILES, D])
        ht = sb("ht", [P, 2, KB, SEQ], F16)
        pad = sb("conv_pad", [P, XBC, TAPS - 1 + SEQ])
        xbc = sb("xbc", [P, XBC, SEQ])
        sz = sb("silu_z", [P, H, SEQ])
        tok = sb("tok", [P, 3, P])
        stats_a = sb("stats_a", [P, TILES, 6])
        mv_a = sb("mv_a", [P, TILES, 2])
        s_a = sb("small_a", [P, 2, TILES])
        dts = sb("dts", [P, 6, TILES, H])
        a_t = sb("a_t", [P, TILES, H])
        ra = sb("ra", [P, TILES, H, P])
        dec = sb("dec", [P, TILES, H, P])
        w0 = sb("w0", [P, H])
        tdt = hn[:].rearrange("p t (h q) -> p t h q", h=H)
        xw = hn[:, 0].rearrange("p (h q) -> p h q", h=H)
        ce = hn[:, 1].rearrange("p (h q) -> p h q", h=H)
        y = sb("y", [P, H, SEQ])
        ss = sb("sumsq", [P, 2, TILES])
        h2t = sb("h2t", [P, 2, KB, SEQ], F16)
        h1b = sb("h1b", [P, TILES, D])
        sg = sb("sg", [P, 2, SEQ])
        act = sb("act", [P, 4, 2, SEQ], F16)
        mlp = sb("mlp", [P, TILES, D])
        x1 = sb("x1", [P, TILES, D])
        h3 = sb("h3", [P, TILES, D])
        h3t = sb("h3t", [P, 2, KB, SEQ], F16)
        scaled_d, scaled_p = mlp, h3
        norms = x1[:, 0, 0:UNITS]
        mabs = x1[:, 0, UNITS:UNITS + 2 * KB].rearrange("p (n k) -> p n k", k=KB)
        gl_raw = x1[:, 0, P:P + KB * (E + E * R)].rearrange("p (k n) -> p k n", k=KB)
        lora_raw, lora_rest = x1[:, 1], h3[:, 1]
        square = h3t[:].rearrange("p s k q -> p (s k q)").bitcast(F32)
        stats_c = sb("stats_c", [P, TILES, 6])
        mv_c = sb("mv_c", [P, TILES, 2])
        s_c = sb("small_c", [P, TILES])
        lg = sb("logits", [P, TILES, E])
        zs = sb("zs", [P, TILES, E * R])
        zr = sb("zr", [P, TILES, E * R])
        zp = sb("z_parts", [P, TILES, 6, E * R], BF16)
        mx = sb("mx", [P, TILES])
        eq = sb("eq", [P, TILES, E])
        seen = sb("seen", [P, TILES, E])
        hot = sb("hot", [P, TILES, E])
        zt_1 = sb("zt_1", [4 * E * R, SEQ], BF16)
        zt_2 = sb("zt_2", [2 * E * R, SEQ], BF16)

        def upper(t):
            return t.bitcast(BF16).rearrange("p (n two) -> p n two", two=2)[:, :, 1]

        GU = [ps("gu0"), ps("gu1")]
        ACC = [ps("acc0"), ps("acc1")]
        WA = [ps("wa0"), ps("wa1"), ps("wa2")]
        WC = ps("wc")

        T_IN, T_GATE, T_UP, T_DOWN, T_LIN, T_GL, T_DT = range(7)
        inv_in, inv_gate, inv_up = sc[:, T_IN, 4:5], sc[:, T_GATE, 4:5], sc[:, T_UP, 4:5]
        inv_lin, inv_gl, inv_dt = sc[:, T_LIN, 4:5], sc[:, T_GL, 4:5], sc[:, T_DT, 4:5]
        act_scale = bound[:, 0:1]
        up_to_act = bound[:, 1:2]
        inv_down = bound[:, 2:3]
        lora_scale = bound[:, 3:4]
        ln_scale = bound[:, 4:6]

        PIECES = [(0, 2), (2, 4), (4, 6), (6, 8), (8, 10), (10, 14)]
        for base in (U_GATE, U_UP, U_DOWN):
            PIECES += [(base + a, min(base + a + 4, base + FBLK)) for a in range(0, FBLK, 4)]
        PIECES += [(U_LIN, UNITS)]
        SOURCES = [(U_IN, w_in), (U_OUT, w_out), (U_GATE, w_gate), (U_UP, w_up), (U_DOWN, w_down),
                   (U_LIN, w_lin)]

        def piece_of(u):
            return next(n for n, (a, b) in enumerate(PIECES) if a <= u < b)

        UNITS_OF = {T_IN: range(U_IN, U_OUT), T_GATE: range(U_GATE, U_UP), T_UP: range(U_UP, U_DOWN),
                    T_DOWN: range(U_DOWN, U_LIN), T_LIN: range(U_LIN, UNITS)}

        def pieces_of(t):
            return sorted({piece_of(u) for u in UNITS_OF[t]})

        def piecewise(kind, t):
            return [(kind, t, n) for n in pieces_of(t)]

        in_order = {}

        def at(step, f, *jobs):
            in_order.setdefault((step, f), []).extend(jobs)

        def split(t, *fs):
            return ("split", t, [UNITS_OF[t][f] for f in fs])

        for n in pieces_of(T_IN):
            at(0, 0, ("gram", T_IN, n), ("norms", T_IN, n))
        at(0, 0, ("max", T_IN, None), ("scale", T_IN, None), split(T_IN, 0, 1))
        at(0, 2, ("max", T_DT, None), split(T_IN, 2, 3, 4, 5), ("small", T_DT, None))
        at(0, 3, *piecewise("gram", T_GATE), split(T_IN, 6, 7, 8, 9))
        at(0, 4, *piecewise("norms", T_GATE), ("max", T_GATE, None))
        at(0, 5, *piecewise("gram", T_UP), ("scale", T_GATE, None), split(T_GATE, 0, 1))
        at(0, 6, *piecewise("norms", T_UP), ("max", T_UP, None), split(T_GATE, 2, 3), ("scale", T_UP, None))
        at(0, 7, *piecewise("gram", T_DOWN), split(T_UP, 0, 1))
        at(0, 8, split(T_UP, 2))
        at(0, 9, split(T_UP, 3), split(T_GATE, 4, 5))
        at(0, 10, split(T_UP, 4, 5))
        at(0, 11, *piecewise("norms", T_DOWN), ("max", T_DOWN, None))
        at(0, 13, split(T_GATE, 6))
        at(1, 0, ("scale", T_DOWN, None), split(T_DOWN, 0))
        at(1, 1, split(T_UP, 6), split(T_DOWN, 1), split(T_GATE, 7), split(T_UP, 7))
        for f in range(2, 8):
            at(1, f, split(T_GATE, f + 6), split(T_UP, f + 6), split(T_DOWN, f))
        at(1, 8, split(T_DOWN, 8, 9, 10))
        at(1, 9, split(T_DOWN, 11, 12, 13))
        at(1, 8, *piecewise("gram", T_LIN))
        at(1, 9, *piecewise("norms", T_LIN), ("max", T_LIN, None), ("max", T_GL, None))
        at(1, 10, ("scale", T_LIN, None), split(T_LIN, 0, 1))
        at(1, 11, split(T_LIN, 2, 3))
        at(1, 12, ("small", T_GL, None))
        at(1, 13, ("lora", None, None))

        order = [u for key in sorted(in_order) for kind, _, us in in_order[key] if kind == "split" for u in us]
        path = {u: "p" if n % 3 == 2 else "d" for n, u in enumerate(order)}
        rank = {u: sum(path[v] == path[u] for v in order[:n]) for n, u in enumerate(order)}
        split_count = {p: sum(q == p for q in path.values()) for p in "dp"}
        scale_order = [t for key in sorted(in_order) for kind, t, _ in in_order[key] if kind == "max"]
        piece_order = [n for key in sorted(in_order) for kind, _, n in in_order[key] if kind == "norms"]

        def wait_split(eng, units):
            for p, s in (("d", split_d), ("p", split_p)):
                n = max([rank[u] + 1 for u in units if path[u] == p], default=0)
                if n:
                    eng.wait_ge(s, n)

        def gram_bank(n):
            return WC if n == len(piece_order) - 1 else (GU + ACC)[n % 4]

        def alone(g):
            return isinstance(g, int) and g == GROUPS - 1

        def h3t_bank(g, b):
            return GU[0] if alone(g) and b == 1 else WC

        def u_bank(g, j):
            return ACC[j] if alone(g) else WC

        split_d, split_p, small_split = sem("split_d"), sem("split_p"), sem("small_split")
        s_piece = [sem(f"piece{n}_loaded") for n in range(len(PIECES))]
        small_loaded, lora_loaded = sem("small_loaded"), sem("lora_loaded")
        x_loaded, xc_loaded, stored = sem("x_loaded"), sem("xc_loaded"), sem("stored")
        masks_made = sem("masks_made")

        def prev(g, per, k, eng, s):
            if not (isinstance(g, int) and g == 0):
                eng.wait_ge(s, g * per - per + k)

        block = ctx.enter_context(nc.Block())

        def steps(eng, step):
            step(0, None, None)
            step(1, 0, None)
            step(2, 1, 0)
            with eng.Fori(2, GROUPS - 1) as i:
                step(i + 1, i, i - 1)
            step(None, GROUPS - 1, GROUPS - 2)
            step(None, None, GROUPS - 1)

        @block.sync
        def _(sp):
            def load_piece(n):
                a, b = PIECES[n]
                base, src = max((p for p in SOURCES if p[0] <= a), key=lambda p: p[0])
                v = src[a - base:b - base]
                v = v.rearrange("u p k n -> p u (k n)") if len(src.shape) == 4 else v.rearrange("u p n -> p u n")
                sp.dma_start(W[:, a:b, :], v).then_inc(s_piece[n], 16)

            sp.dma_start(xa[:], x_g[0]).then_inc(x_loaded, 16)
            sp.dma_start(lnt[:].rearrange("p t d -> p (t d)"), ln_rows.broadcast_to([P, 2 * D]))\
                .then_inc(small_loaded, 16)
            sp.dma_start(colt[:], cols).then_inc(small_loaded, 16)
            sp.dma_start(rowt[:], rows.broadcast_to([P, 16])).then_inc(small_loaded, 16)
            sp.dma_start(dt_raw, w_dt).then_inc(small_loaded, 16)
            for n in range(len(PIECES)):
                load_piece(n)
            sp.dma_start(gl_raw, w_gl).then_inc(lora_loaded, 16)
            sp.dma_start(lora_raw, lora_b).then_inc(lora_loaded, 16)

            def step(a, b, c):
                if a is not None and not (isinstance(a, int) and a == 0):
                    sp.wait_ge(sem("h0_ready"), a * 2)
                    sp.dma_start(xa[:], x_g[a]).then_inc(x_loaded, 16)
                if c is not None:
                    prev(c, 32, 32, sp, stored)
                    if isinstance(c, int) and c == 0:
                        sp.wait_ge(sem("lora_split"), 2)
                    sp.dma_start(x1[:], x_g[c]).then_inc(xc_loaded, 16)
                    for j in range(TILES):
                        sp.wait_ge(sem("out_ready"), c * 2 + j + 1)
                        sp.dma_start(out_g[c, j], h3[:, j]).then_inc(stored, 16)

            steps(sp, step)
            sp.wait_ge(stored, 16 * TILES * GROUPS)

        @block.gpsimd
        def _(pool):
            nc.gpsimd.memset(ident[:], 0.0).then_inc(masks_made, 1)
            nc.gpsimd.memset(tri[:], 1.0).then_inc(masks_made, 1)
            nc.gpsimd.memset(below[:], 1.0).then_inc(masks_made, 1)
            nc.gpsimd.memset(ones[:], 1.0).then_inc(masks_made, 1)
            nc.gpsimd.memset(pad[:, :, 0:TAPS - 1], 0.0).then_inc(masks_made, 1)
            nc.gpsimd.memset(minus_half[:], -0.5).then_inc(masks_made, 1)
            pool.wait_ge(masks_made, 6)
            nc.gpsimd.affine_select(out=ident[:], in_=ident[:], compare_op=ALU.not_equal, fill=1.0, base=0,
                                    pattern=[[-1, P]], channel_multiplier=1).then_inc(masks_made, 1)
            nc.gpsimd.affine_select(out=tri[:], in_=tri[:], compare_op=ALU.is_ge, fill=0.0, base=0,
                                    pattern=[[1, P]], channel_multiplier=-1).then_inc(masks_made, 1)
            nc.gpsimd.affine_select(out=below[:], in_=below[:], compare_op=ALU.is_gt, fill=0.0, base=0,
                                    pattern=[[-1, P]], channel_multiplier=1).then_inc(masks_made, 1)
            pool.wait_ge(masks_made, 9)

            def wait_apart(s, value):
                pool.wait_ge(s, value)
                pool.sem_inc(sem("pool_waited"), 1)

            setup = Chain(pool, sem("pool_setup"), 0)
            setup.group(0)

            def prepare(step, f):
                for kind, t, what in in_order.get((step, f), []):
                    if kind == "max":
                        n = scale_order.index(t)
                        pool.wait_ge(sem("norm_ready"), n + 1)
                        setup(nc.gpsimd.partition_all_reduce(sc[:, t, 1:2], sc[:, t, 0:1], P, RMAX))
                        setup(nc.gpsimd.tensor_scalar(sc[:, t, 1:2], sc[:, t, 1:2], TINY ** 2,
                                                      BF_SLACK / TOP ** 2, ALU.max, ALU.mult))
                        nc.gpsimd.tensor_tensor(sc[:, t, 2:3], sc[:, t, 1:2], minus_half[:, 0:1], ALU.pow)\
                            .then_inc(sem("raw_scale_ready"), 1)
                    if kind == "split":
                        for u in what:
                            if path[u] == "p":
                                pool.wait_ge(sem("hi_p"), rank[u] + 1)
                                nc.gpsimd.tensor_tensor(Wh[:, u, 1], scaled_p[:, rank[u] % 2], Wh[:, u, 0],
                                                        ALU.subtract).then_inc(split_p, 1)

            chain_a = Chain(pool, sem("pool_a"), 3, wait_apart)
            chain_c = Chain(pool, sem("pool_c"), 3, wait_apart)

            def inv_std(chain, dst, var, factor, shift, ready):
                chain(nc.gpsimd.tensor_scalar(dst, var, factor, shift, ALU.mult, ALU.add))
                nc.gpsimd.tensor_tensor(dst, dst, minus_half[:], ALU.pow).then_inc(ready, 1)

            def a_norm(g):
                wait_apart(sem("stats_a_ready"), g + 1)
                inv_std(chain_a, s_a[:, 1], mv_a[:, :, 1], 1.0 + EPS, EPS * EPS, sem("rstd2_a_ready"))
                inv_std(chain_a, s_a[:, 0], mv_a[:, :, 1], 1.0, EPS, sem("rstd_a_ready"))

            def a_scan_in(g):
                pool.wait_ge(sem("a_ready"), g + 1)
                for j in range(TILES):
                    if j == 0:
                        prev(g, 3, 3, pool, sem("dec_ps_ready"))
                    nc.gpsimd.tensor_tensor(ra[:, j], tri[:].unsqueeze(1).broadcast_to([P, H, P]),
                                            a_t[:, j].unsqueeze(2).broadcast_to([P, H, P]), ALU.mult)\
                        .then_inc(sem("ra_ready"), 1)

            def a_tdt(g):
                for j in range(TILES):
                    nc.gpsimd.tensor_tensor(tdt[:, j], tri[:].unsqueeze(1).broadcast_to([P, H, P]),
                                            dts[:, 4, j].unsqueeze(2).broadcast_to([P, H, P]), ALU.mult)\
                        .then_inc(sem("tdt_ready"), 1)

            def a_xd(g):
                prev(g, 2, 2, pool, sem("o_ps_ready"))
                wait_apart(sem("xbc_ready"), g * 3 + 1)
                for h in range(H):
                    nc.gpsimd.tensor_scalar(y[:, h], xbc[:, 0], rowt[:, 4 + h:5 + h], None, ALU.mult)\
                        .then_inc(sem("xd_ready"), 1)

            def a_xw(g):
                pool.wait_ge(sem("w0_ready"), g + 1)
                pool.wait_ge(sem("tok_ready"), g + 1)
                prev(g, 2, 2, pool, sem("y_ps_ready"))
                nc.gpsimd.tensor_tensor(xw[:], tok[:, 0].unsqueeze(1).broadcast_to([P, H, P]),
                                        w0[:].unsqueeze(2).broadcast_to([P, H, P]), ALU.mult)\
                    .then_inc(sem("xw_ready"), 1)

            def a_ce(g):
                pool.wait_ge(sem("exp_ready"), g * 3 + 3)
                nc.gpsimd.tensor_tensor(ce[:], ce[:], xbc[:, 2:6, P:SEQ], ALU.mult)\
                    .then_inc(sem("ce_ready"), 1)

            def a_rms(g):
                wait_apart(sem("sumsq_ready"), g * 2 + 2)
                inv_std(chain_a, ss[:, 1], ss[:, 0], 1.0 / D, EPS, sem("rms_ready"))

            def b_copy(g):
                if not (isinstance(g, int) and g == 0):
                    wait_apart(sem("mlp_ready"), g * 2)
                wait_apart(sem("h1_ready"), g * 2 + 2)
                nc.gpsimd.tensor_copy(h1b[:], h01[:]).then_inc(sem("h1b_ready"), 1)

            def norm_c(g, n, scale):
                wait_apart(sem("stats_c_ready"), g * 3 + n)
                inv_std(chain_c, s_c[:], mv_c[:, :, 1], 1.0 / scale ** 2, EPS / scale ** 2,
                        sem("rstd_c_ready"))

            def step(a, b, c):
                if a is not None:
                    chain_a.group(a)
                if c is not None:
                    chain_c.group(c)
                if a is not None:
                    a_norm(a)
                if isinstance(a, int) and a == 0:
                    prepare(0, 0)
                if c is not None:
                    norm_c(c, 1, 1.0)
                    norm_c(c, 2, ACT_SCALE)
                if b is not None:
                    b_copy(b)

                def prepare_at(*blocks):
                    for f in blocks if isinstance(a, int) and a <= 1 else []:
                        prepare(a, f)

                if isinstance(a, int) and a == 1:
                    prepare(1, 0)
                prepare_at(1, 2, 3)
                if a is not None:
                    a_xd(a)
                prepare_at(4, 5)
                if a is not None:
                    a_scan_in(a)
                    a_tdt(a)
                prepare_at(6, 7)
                if a is not None:
                    a_xw(a)
                prepare_at(8)
                if a is not None:
                    a_ce(a)
                prepare_at(9, 10, 11)
                if c is not None:
                    norm_c(c, 3, 1.0)
                if a is not None:
                    a_rms(a)
                    chain_a.close()
                prepare_at(12, 13)
                if c is not None:
                    chain_c.close()

            steps(pool, step)

        @block.scalar
        def _(eng):
            chain_a = Chain(eng, sem("act_a"), 2)

            def prep_a():
                eng.wait_ge(small_loaded, 64)
                nc.scalar.activation(neg_a[:], rowt[:, 0:4], ACT.Exp).then_inc(sem("exp_a_log"), 1)

            scaling = Chain(eng, sem("act_scaling"), 0)
            scaling.group(0)

            def prepare(step, f):
                for kind, t, what in in_order.get((step, f), []):
                    if kind == "small":
                        raw, w = (dt_raw, dt_w) if t == T_DT else (gl_raw, gl_w)
                        eng.wait_ge(sem("small_scaled"), 1 + (t == T_GL))
                        nc.scalar.activation(w[:, 0], raw, ACT.Copy).then_inc(sem("small_hi"), 1)
                    for u in what if kind == "split" else []:
                        n = rank[u]
                        if path[u] == "p":
                            eng.wait_ge(sem("scale_ready"), scale_order.index(t) + 1)
                            if n >= 2:
                                eng.wait_ge(split_p, n - 1)
                            scaling(nc.scalar.activation(scaled_p[:, n % 2], W[:, u], ACT.Copy,
                                                         scale=sc[:, t, 3:4]))
                            nc.scalar.activation(Wh[:, u, 0], scaled_p[:, n % 2], ACT.Copy)\
                                .then_inc(sem("hi_p"), 1)
                        else:
                            eng.wait_ge(sem("scaled_d_ready"), n + 1)
                            nc.scalar.activation(Wh[:, u, 0], scaled_d[:, n % 2], ACT.Copy)\
                                .then_inc(sem("hi_d"), 1)

            def a_t1(g):
                for b in range(2):
                    eng.wait_ge(sem("ht_ps_ready"), g * 2 + b + 1)
                    prev(g, 2, 2, eng, sem("z_ps_ready"))
                    nc.scalar.activation(ht[:, 0, 2 * b:2 * b + 2].rearrange("p k s -> p (k s)"),
                                         WA[b][:], ACT.Copy).then_inc(sem("ht_hi"), 1)

            XB_BANK = [2, 0, 1]

            def a_conv(g, b):
                eng.wait_ge(sem("xbc_ps_ready"), g * 3 + b + 1)
                src = WA[XB_BANK[b]]
                if b == 0:
                    prev(g, 3, 3, eng, sem("dec_ps_ready"))
                    prev(g, 2, 2, eng, sem("att_ps_ready"))
                    prev(g, 1, 1, eng, sem("ce_ready"))
                    prev(g, 4, 4, eng, sem("xd_ready"))
                for m in range(2):
                    c = 2 * b + m
                    nc.scalar.activation(xbc[:, c], src[:, m * SEQ:(m + 1) * SEQ], ACT.Identity,
                                         bias=conv_b[:, c:c + 1],
                                         scale=cw[:, c * TAPS + TAPS - 1:c * TAPS + TAPS])\
                        .then_inc(sem("tap_ready"), 1)
                nc.scalar.activation(pad[:, 2 * b:2 * b + 2, TAPS - 1:],
                                     src[:].rearrange("p (m s) -> p m s", m=2), ACT.Copy)\
                    .then_inc(sem("pad_ready"), 1)

            def a_silu(g, b):
                eng.wait_ge(sem("conv_ready"), g * XBC + 2 * b + 2)
                nc.scalar.activation(xbc[:, 2 * b:2 * b + 2], xbc[:, 2 * b:2 * b + 2], ACT.Silu)\
                    .then_inc(sem("xbc_ready"), 1)

            def a_z(g, b):
                eng.wait_ge(sem("z_ps_ready"), g * 2 + b + 1)
                prev(g, 2, 2, eng, sem("y_ready"))
                nc.scalar.activation(sz[:, 2 * b:2 * b + 2], WA[b][:].rearrange("p (m s) -> p m s", m=2),
                                     ACT.Silu, scale=inv_in).then_inc(sem("sz_ready"), 1)

            def a_dt(g):
                eng.wait_ge(sem("dtv_ready"), g + 1)
                chain_a(nc.scalar.activation(dts[:, 1], dts[:, 0], ACT.Abs))
                chain_a(nc.scalar.activation(dts[:, 2], dts[:, 1], ACT.Exp, scale=-1.0))
                nc.scalar.activation(dts[:, 3], dts[:, 2], ACT.Ln, bias=1.0).then_inc(sem("log_ready"), 1)

            def a_tok(g):
                eng.wait_ge(sem("tok_ps_ready"), g + 1)
                prev(g, 2, 2, eng, sem("y_ps_ready"))
                nc.scalar.activation(tok[:].rearrange("p m s -> p (m s)"), WA[2][:, 0:3 * P], ACT.Copy)\
                    .then_inc(sem("tok_ready"), 1)

            def a_exp(g, n):
                eng.wait_ge(sem("dec_ps_ready"), g * 3 + n + 1)
                if n == 0:
                    prev(g, 2, 2, eng, sem("y_ps_ready"))
                if n == 2:
                    eng.wait_ge(sem("decdt_ready"), g * 2 + 2)
                dst = dec[:, n] if n < TILES else ce[:]
                nc.scalar.activation(dst.rearrange("p h q -> p (h q)"), WA[[0, 1, 0][n]][:], ACT.Exp)\
                    .then_inc(sem("exp_ready"), 1)

            def a_state(g):
                eng.wait_ge(sem("st_ps_ready"), g + 1)
                nc.scalar.activation(xw[:].rearrange("p h q -> p (h q)"), WA[2][:], ACT.Copy)\
                    .then_inc(sem("state_ready"), 1)

            def a_sumsq(g, j):
                eng.wait_ge(sem("h1_ready"), g * 2 + j + 1)
                if j == 0:
                    prev(g, 2, 2, eng, sem("h2t_ps_ready"))
                nc.scalar.activation(hn[:, j], h01[:, j], ACT.Square, accum_out=ss[:, 0, j:j + 1])\
                    .then_inc(sem("sumsq_ready"), 1)

            def a_t2(g):
                for b in range(2):
                    eng.wait_ge(sem("h2t_ps_ready"), g * 2 + b + 1)
                    prev(g, FBLK, FBLK, eng, sem("gu_ready"))
                    nc.scalar.activation(h2t[:, 0, 2 * b:2 * b + 2].rearrange("p k s -> p (k s)"),
                                         WA[1 + b][:], ACT.Copy).then_inc(sem("h2t_hi"), 1)

            def b_silu(g, f):
                eng.wait_ge(sem("gu_ready"), g * FBLK + f + 1)
                if f >= 2:
                    eng.wait_ge(sem("act_ready"), g * FBLK + f - 1)
                else:
                    prev(g, FBLK, FBLK - 1 + f, eng, sem("act_ready"))
                nc.scalar.activation(sg[:, f % 2], GU[f % 2][:, 0:SEQ], ACT.Silu, scale=inv_gate)\
                    .then_inc(sem("sg_ready"), 1)

            def b_hi(g, f):
                eng.wait_ge(sem("prod_ready"), g * FBLK + f + 1)
                if f >= 4:
                    eng.wait_ge(sem("down_done"), g * FBLK + f - 3)
                else:
                    prev(g, FBLK, last_in_slot(f) + 1, eng, sem("down_done"))
                nc.scalar.activation(act[:, slot(f), 0], sg[:, f % 2], ACT.Copy)\
                    .then_inc(sem("act_hi"), 1)

            def c_t3(g, b):
                eng.wait_ge(sem("h3t_ps_ready"), g * 2 + b + 1)
                prev(g, 2, 2, eng, sem("u_ps_ready"))
                nc.scalar.activation(h3t[:, 0, 2 * b:2 * b + 2].rearrange("p k s -> p (k s)"),
                                     h3t_bank(g, b)[:], ACT.Copy).then_inc(sem("h3t_hi"), 1)

            def c_zt(g):
                eng.wait_ge(sem("zt_ps_ready"), g + 1)
                prev(g, 2, 2, eng, sem("u_ps_ready"))
                bank = WC[:].bitcast(BF16)
                nc.scalar.activation(zt_1[:], bank[:, 0:SEQ], ACT.Copy).then_inc(sem("zt_ready"), 1)
                nc.scalar.activation(zt_2[:], bank[0:2 * E * R, SEQ:2 * SEQ], ACT.Copy).then_inc(sem("zt_ready"), 1)

            def c_u(g, j):
                eng.wait_ge(sem("u_ps_ready"), g * 2 + j + 1)
                nc.scalar.activation(h3[:, j], u_bank(g, j)[:], ACT.Copy, scale=inv_lin).then_inc(sem("u_ready"), 1)

            A_AT = {1: lambda g: a_t1(g), 2: lambda g: a_conv(g, 0),
                    3: lambda g: (a_conv(g, 1), a_conv(g, 2), a_silu(g, 0)),
                    4: lambda g: (a_silu(g, 1), a_z(g, 0), a_dt(g)),
                    5: lambda g: (a_silu(g, 2), a_z(g, 1), a_tok(g)),
                    6: lambda g: (a_exp(g, 0), a_exp(g, 1)), 8: lambda g: (a_exp(g, 2), a_state(g)),
                    10: lambda g: a_sumsq(g, 0), 11: lambda g: a_sumsq(g, 1), 13: lambda g: a_t2(g)}
            C_AT = {4: lambda g: c_t3(g, 0), 5: lambda g: c_t3(g, 1), 7: lambda g: c_zt(g),
                    8: lambda g: c_u(g, 0), 9: lambda g: c_u(g, 1)}

            def step(a, b, c):
                if a is not None:
                    chain_a.group(a)
                if isinstance(a, int) and a == 0:
                    prep_a()
                for f in range(FBLK):
                    if isinstance(a, int) and a <= 1:
                        prepare(a, f)
                    if b is not None:
                        b_silu(b, f)
                        b_hi(b, f)
                    if a is not None and f in A_AT:
                        A_AT[f](a)
                    if c is not None and f in C_AT:
                        C_AT[f](c)
                if a is not None:
                    chain_a.close()

            steps(eng, step)

        @block.vector
        def _(dve):
            setup = Chain(dve, sem("dve_setup"), 0)
            setup.group(0)

            def wait_apart(s, value):
                dve.wait_ge(s, value)
                dve.sem_inc(sem("dve_waited"), 1)

            chain_a = Chain(dve, sem("dve_a"), 20, wait_apart)
            chain_c = Chain(dve, sem("dve_c"), 19, wait_apart)

            def scale_done(t, products):
                s = sc[:, t]
                dve.wait_ge(sem("raw_scale_ready"), scale_order.index(t) + 1)
                nc.vector.tensor_single_scalar(s[:, 3:4].bitcast(I32), s[:, 2:3].bitcast(I32), POW2,
                                               ALU.bitwise_and).then_inc(sem("scale_ready"), 1)
                dve.wait_ge(sem("scale_ready"), scale_order.index(t) + 1)
                setup(nc.vector.reciprocal(s[:, 4:5], s[:, 3:4]))
                setup(nc.vector.tensor_scalar(s[:, 4:5], s[:, 4:5], products, None, ALU.mult))

            def ln_row(n):
                m, r = bound[:, 6 + n:7 + n], bound[:, 8 + n:9 + n]
                setup(nc.vector.tensor_reduce(m, lnt[:, n], AX.X, ALU.max, apply_absolute_value=True))
                setup(nc.vector.tensor_scalar(m, m, TINY, ROOT_D / TOP, ALU.max, ALU.mult))
                setup(nc.vector.reciprocal(r, m))
                setup(nc.vector.tensor_single_scalar(ln_scale[:, n:n + 1].bitcast(I32), r.bitcast(I32), POW2,
                                                     ALU.bitwise_and))
                setup(nc.vector.reciprocal(m, ln_scale[:, n:n + 1]))
                setup(nc.vector.tensor_scalar(lnt[:, n], lnt[:, n], ln_scale[:, n:n + 1], None, ALU.mult))

            inv_ln = [bound[:, 6:7], bound[:, 7:8]]

            def prep_norms(n):
                a, b = PIECES[n]
                bank = gram_bank(piece_order.index(n))
                dve.wait_ge(sem("gram_ready"), piece_order.index(n) + 1)
                for u in range(a, b):
                    ins = nc.vector.tensor_tensor_reduce(
                        out=square[:, (u - a) * P:(u - a + 1) * P], in0=bank[:, (u - a) * P:(u - a + 1) * P],
                        in1=ident[:], scale=1.0, scalar=0.0, op0=ALU.mult, op1=ALU.add,
                        accum_out=norms[:, u:u + 1])
                    if u == b - 1:
                        ins.then_inc(sem("gram_read"), 1)
                dve.wait_ge(sem("gram_read"), piece_order.index(n) + 1)

            def prep_max(t):
                if t not in UNITS_OF:
                    raw, n = (dt_raw, 0) if t == T_DT else (gl_raw, 1)
                    dve.wait_ge(*((small_loaded, 64) if t == T_DT else (lora_loaded, 32)))
                    setup(nc.vector.tensor_reduce(mabs[:, n], raw, AX.X, ALU.max, apply_absolute_value=True))
                    setup(nc.vector.tensor_tensor(mabs[:, n], mabs[:, n], mabs[:, n], ALU.mult))
                    nc.vector.tensor_reduce(sc[:, t, 0:1], mabs[:, n], AX.X, ALU.max).then_inc(sem("norm_ready"), 1)
                    return
                us = UNITS_OF[t]
                nc.vector.tensor_reduce(sc[:, t, 0:1], norms[:, us[0]:us[-1] + 1], AX.X, ALU.max)\
                    .then_inc(sem("norm_ready"), 1)

            def prep_scale(t):
                scale_done(t, {T_IN: inv_ln[0], T_GATE: inv_ln[1], T_UP: inv_ln[1], T_DOWN: 1.0,
                               T_LIN: 1.0 / ACT_SCALE}[t])
                if t == T_IN:
                    setup(nc.vector.tensor_scalar(cw[:], conv_w, inv_in, None, ALU.mult))
                    dve.wait_ge(sem("exp_a_log"), 1)
                    setup(nc.vector.tensor_scalar(neg_a[:], neg_a[:], -1.0, None, ALU.mult))
                if t == T_UP:
                    setup(nc.vector.tensor_scalar(act_scale, inv_gate, 2.0 ** 45, inv_up, ALU.mult, ALU.mult))
                    setup(nc.vector.reciprocal(act_scale, act_scale))
                    setup(nc.vector.tensor_scalar(up_to_act, act_scale, inv_up, None, ALU.mult))
                if t == T_DOWN:
                    setup(nc.vector.reciprocal(inv_down, act_scale))
                    setup(nc.vector.tensor_scalar(inv_down, inv_down, sc[:, t, 4:5], None, ALU.mult))

            def prep_small(t):
                raw, w, n = (dt_raw, dt_w, 0) if t == T_DT else (gl_raw, gl_w, 1)
                scale_done(t, inv_ln[0] if t == T_DT else 1.0 / ACT_SCALE)
                nc.vector.tensor_scalar(raw, raw, sc[:, t, 3:4], None, ALU.mult)\
                    .then_inc(sem("small_scaled"), 1)
                if t == T_GL:
                    setup(nc.vector.tensor_scalar(lora_scale, inv_gl, sc[:, T_LIN, 3:4], ACT_SCALE,
                                                  ALU.mult, ALU.mult))
                dve.wait_ge(sem("small_hi"), 1 + n)
                nc.vector.tensor_tensor(w[:, 1], raw, w[:, 0], ALU.subtract).then_inc(small_split, 1)

            def prep_lora():
                n = E * R
                dve.wait_ge(split_p, split_count["p"])
                setup(nc.vector.tensor_copy(lora_1[:], lora_raw))
                setup(nc.vector.tensor_tensor(lora_rest, lora_raw, lora_1[:], ALU.subtract))
                setup(nc.vector.tensor_copy(lora_2[0:n], lora_rest[0:n]))
                setup(nc.vector.tensor_tensor(lora_2[0:n], lora_rest[0:n], lora_2[0:n], ALU.subtract))
                setup(nc.vector.tensor_copy(lora_2[n:2 * n], lora_raw[n:2 * n]))
                for m in (1, 3):
                    nc.vector.tensor_copy(lora_1[m * n:(m + 1) * n], lora_rest[m * n:(m + 1) * n])\
                        .then_inc(sem("lora_split"), 1)

            def prep_split(t, units):
                units = [u for u in units if path[u] == "d"]

                def lo(u):
                    n = rank[u]
                    dve.wait_ge(sem("hi_d"), n + 1)
                    nc.vector.tensor_tensor(Wh[:, u, 1], scaled_d[:, n % 2], Wh[:, u, 0], ALU.subtract)\
                        .then_inc(split_d, 1)

                for m, u in enumerate(units):
                    n = rank[u]
                    if n >= 2:
                        dve.wait_ge(split_d, n - 1)
                    nc.vector.tensor_scalar(scaled_d[:, n % 2], W[:, u], sc[:, t, 3:4], None, ALU.mult)\
                        .then_inc(sem("scaled_d_ready"), 1)
                    if m:
                        lo(units[m - 1])
                if units:
                    lo(units[-1])

            def prepare(step, f):
                for kind, t, what in in_order.get((step, f), []):
                    {"gram": lambda: None, "norms": lambda: prep_norms(what), "max": lambda: prep_max(t), "scale": lambda: prep_scale(t),
                     "small": lambda: prep_small(t), "lora": prep_lora,
                     "split": lambda: prep_split(t, what)}[kind]()

            def stats(chain, src, st, mv, done):
                for j in range(TILES):
                    chain(nc.vector.bn_stats(st[:, j], src[:, j]), wait=j == TILES - 1)
                chain(nc.vector.bn_aggr(mv[:, 0], st[:, 0]), wait=False)
                nc.vector.bn_aggr(mv[:, 1], st[:, 1]).then_inc(done, 1)

            def a_stats(g):
                dve.wait_ge(x_loaded, g * 16 + 16)
                prev(g, 1, 1, dve, sem("rstd_a_ready"))
                stats(chain_a, xa, stats_a, mv_a, sem("stats_a_ready"))

            def a_center(g):
                prev(g, 2, 2, dve, sem("h2t_ps_ready"))
                dve.wait_ge(sem("stats_a_ready"), g + 1)
                for j in range(TILES):
                    nc.vector.scalar_tensor_tensor(hn[:, j], xa[:, j], mv_a[:, j, 0:1], lnt[:, 0],
                                                   ALU.subtract, ALU.mult).then_inc(sem("centered"), 1)

            def a_norm(g):
                dve.wait_ge(sem("rstd2_a_ready"), g + 1)
                for j in range(TILES):
                    dve.wait_ge(sem("centered"), g * 2 + j + 1)
                    nc.vector.tensor_scalar(hn[:, j], hn[:, j], s_a[:, 1, j:j + 1], None, ALU.mult)\
                        .then_inc(sem("hn_ready"), 1)

            def a_h0(g):
                dve.wait_ge(sem("rstd_a_ready"), g + 1)
                prev(g, 1, 1, dve, sem("h1b_ready"))
                for j in range(TILES):
                    nc.vector.tensor_scalar(h01[:, j], xa[:, j], mv_a[:, j, 0:1], s_a[:, 0, j:j + 1],
                                            ALU.subtract, ALU.mult).then_inc(sem("h0_ready"), 1)

            def a_t1(g):
                for b in range(2):
                    dve.wait_ge(sem("ht_hi"), g * 2 + b + 1)
                    nc.vector.tensor_tensor(ht[:, 1, 2 * b:2 * b + 2].rearrange("p k s -> p (k s)"), WA[b][:],
                                            ht[:, 0, 2 * b:2 * b + 2].rearrange("p k s -> p (k s)"),
                                            ALU.subtract).then_inc(sem("ht_ready"), 1)

            def a_conv(g, b):
                dve.wait_ge(sem("pad_ready"), g * 3 + b + 1)
                for k in range(TAPS - 1):
                    for m in range(2):
                        c = 2 * b + m
                        ins = nc.vector.scalar_tensor_tensor(
                            xbc[:, c], pad[:, c, k:k + SEQ], cw[:, c * TAPS + k:c * TAPS + k + 1],
                            xbc[:, c], ALU.mult, ALU.add)
                        if k == TAPS - 2:
                            ins.then_inc(sem("conv_ready"), 1)
                        elif m == 1:
                            chain_a(ins)
                        else:
                            ins.then_inc(sem("conv_part"), 1)
                    if k < TAPS - 2:
                        dve.wait_ge(sem("conv_part"), g * 6 + b * 2 + k + 1)

            def a_dtv(g):
                dve.wait_ge(sem("dt_ps_ready"), g + 1)
                nc.vector.scalar_tensor_tensor(
                    dts[:, 0], WA[2][:, 0:TILES * H].rearrange("p (t h) -> p t h", h=H), inv_dt,
                    rowt[:, 8:12].unsqueeze(1).broadcast_to([P, TILES, H]), ALU.mult, ALU.add)\
                    .then_inc(sem("dtv_ready"), 1)

            def a_dt(g):
                dve.wait_ge(sem("log_ready"), g + 1)
                v, e, log, t, s = dts[:, 0], dts[:, 2], dts[:, 3], dts[:, 1], dts[:, 5]
                chain_a(nc.vector.tensor_scalar(t, e, 0.2, -0.25, ALU.mult, ALU.add))
                for c in (0.0, 1.0 / 3, -0.5, 1.0):
                    if c:
                        chain_a(nc.vector.scalar_tensor_tensor(t, t, c, e, ALU.add, ALU.mult))
                    else:
                        chain_a(nc.vector.tensor_tensor(t, t, e, ALU.mult))
                chain_a(nc.vector.tensor_tensor(t, t, log, ALU.subtract))
                chain_a(nc.vector.scalar_tensor_tensor(s, e, SERIES, t, ALU.is_lt, ALU.mult))
                chain_a(nc.vector.tensor_tensor(s, s, log, ALU.add))
                chain_a(nc.vector.scalar_tensor_tensor(dts[:, 4], v, 0.0, s, ALU.max, ALU.add))
                nc.vector.tensor_tensor(a_t[:], dts[:, 4], neg_a[:].unsqueeze(1).broadcast_to([P, TILES, H]),
                                        ALU.mult).then_inc(sem("a_ready"), 1)

            def flat(t):
                return t.rearrange("p h q -> p (h q)")

            def a_dec(g, j):
                dve.wait_ge(sem("exp_ready"), g * 3 + j + 1)
                dve.wait_ge(sem("tdt_ready"), g * 2 + j + 1)
                nc.vector.tensor_tensor(flat(dec[:, j]), flat(dec[:, j]), flat(tdt[:, j]), ALU.mult)\
                    .then_inc(sem("decdt_ready"), 1)
                dve.wait_ge(sem("decdt_ready"), g * 2 + j + 1)
                if j == 0:
                    nc.vector.tensor_copy(w0[:], dec[:, 0, :, P - 1]).then_inc(sem("w0_ready"), 1)
                    dve.wait_ge(sem("w0_ready"), g + 1)

            def a_att(g, j):
                dve.wait_ge(sem("att_ps_ready"), g * 2 + j + 1)
                nc.vector.tensor_tensor(flat(dec[:, j]), flat(dec[:, j]), WA[[2, 1][j]][:], ALU.mult)\
                    .then_inc(sem("attw_ready"), 1)

            def a_y(g, j):
                dve.wait_ge(sem("y_ps_ready"), g * 2 + j + 1)
                dve.wait_ge(sem("xd_ready"), g * 4 + 4)
                dve.wait_ge(sem("sz_ready"), g * 2 + 2)
                q = slice(j * P, j * P + P)
                chain_a(nc.vector.tensor_tensor(y[:, :, q], WA[j][:].rearrange("p (h q) -> p h q", h=H),
                                                y[:, :, q], ALU.add))
                nc.vector.tensor_tensor(y[:, :, q], y[:, :, q], sz[:, :, q], ALU.mult)\
                    .then_inc(sem("y_ready"), 1)

            def a_h1(g, j):
                dve.wait_ge(sem("o_ps_ready"), g * 2 + j + 1)
                nc.vector.tensor_tensor(h01[:, j], WA[[2, 0][j]][:], h01[:, j], ALU.add)\
                    .then_inc(sem("h1_ready"), 1)

            def a_h2(g, j):
                dve.wait_ge(sem("rms_ready"), g + 1)
                nc.vector.scalar_tensor_tensor(hn[:, j], h01[:, j], ss[:, 1, j:j + 1], lnt[:, 1],
                                               ALU.mult, ALU.mult).then_inc(sem("h2_ready"), 1)

            def a_t2(g):
                for b in range(2):
                    dve.wait_ge(sem("h2t_hi"), g * 2 + b + 1)
                    nc.vector.tensor_tensor(h2t[:, 1, 2 * b:2 * b + 2].rearrange("p k s -> p (k s)"), WA[1 + b][:],
                                            h2t[:, 0, 2 * b:2 * b + 2].rearrange("p k s -> p (k s)"),
                                            ALU.subtract).then_inc(sem("h2t_ready"), 1)

            def b_prod(g, f):
                dve.wait_ge(sem("sg_ready"), g * FBLK + f + 1)
                nc.vector.scalar_tensor_tensor(sg[:, f % 2], GU[f % 2][:, SEQ:2 * SEQ], up_to_act, sg[:, f % 2],
                                               ALU.mult, ALU.mult).then_inc(sem("prod_ready"), 1)

            def b_lo(g, f):
                dve.wait_ge(sem("act_hi"), g * FBLK + f + 1)
                nc.vector.tensor_tensor(act[:, slot(f), 1], sg[:, f % 2], act[:, slot(f), 0], ALU.subtract)\
                    .then_inc(sem("act_ready"), 1)

            def b_mlp(g):
                dve.wait_ge(sem("h1b_ready"), g + 1)
                for j in range(TILES):
                    if j == 0:
                        dve.wait_ge(sem("acc0_ready"), g + 1)
                    else:
                        dve.wait_ge(sem("down_done"), g * FBLK + FBLK)
                    nc.vector.scalar_tensor_tensor(mlp[:, j], ACC[j][:], inv_down, h1b[:, j], ALU.mult, ALU.add)\
                        .then_inc(sem("mlp_ready"), 1)

            def c_stats1(g):
                dve.wait_ge(sem("mlp_ready"), g * 2 + 2)
                prev(g, 3, 3, dve, sem("rstd_c_ready"))
                stats(chain_c, mlp, stats_c, mv_c, sem("stats_c_ready"))

            def c_norm(g, n, src, dst, ready):
                dve.wait_ge(sem("rstd_c_ready"), g * 3 + n)
                for j in range(TILES):
                    nc.vector.tensor_scalar(dst[:, j], src[:, j], mv_c[:, j, 0:1], s_c[:, j:j + 1],
                                            ALU.subtract, ALU.mult).then_inc(ready, 1)

            def c_x1(g):
                prev(g, 32, 32, dve, stored)
                c_norm(g, 1, mlp, h3, sem("n1_ready"))
                dve.wait_ge(xc_loaded, g * 16 + 16)
                for j in range(TILES):
                    dve.wait_ge(sem("n1_ready"), g * 2 + j + 1)
                    nc.vector.tensor_tensor(x1[:, j], x1[:, j], h3[:, j], ALU.add).then_inc(sem("x1_ready"), 1)

            def c_stats2(g):
                dve.wait_ge(sem("x1_ready"), g * 2 + 2)
                stats(chain_c, x1, stats_c, mv_c, sem("stats_c_ready"))

            def c_h3(g):
                c_norm(g, 2, x1, h3, sem("h3_ready"))

            def c_t3(g, b):
                dve.wait_ge(sem("h3t_hi"), g * 2 + b + 1)
                nc.vector.tensor_tensor(h3t[:, 1, 2 * b:2 * b + 2].rearrange("p k s -> p (k s)"), h3t_bank(g, b)[:],
                                        h3t[:, 0, 2 * b:2 * b + 2].rearrange("p k s -> p (k s)"),
                                        ALU.subtract).then_inc(sem("h3t_ready"), 1)

            def c_route(g):
                dve.wait_ge(sem("lg_ps_ready"), g + 1)
                src = WC[:, 0:TILES * (E + E * R)].rearrange("p (t n) -> p t n", t=TILES)
                chain_c(nc.vector.scalar_tensor_tensor(
                    lg[:], src[:, :, 0:E], inv_gl, rowt[:, 12:16].unsqueeze(1).broadcast_to([P, TILES, E]),
                    ALU.mult, ALU.add))
                nc.vector.tensor_scalar(zs[:], src[:, :, E:], lora_scale, None, ALU.mult)\
                    .then_inc(sem("zs_ready"), 1)
                chain_c(nc.vector.tensor_reduce(mx[:], lg[:], AX.X, ALU.max))
                chain_c(nc.vector.tensor_tensor(eq[:], lg[:], mx[:].unsqueeze(2).broadcast_to([P, TILES, E]),
                                                ALU.is_equal))
                chain_c(nc.vector.tensor_copy(seen[:, :, 0:1], eq[:, :, 0:1]))
                for e in range(1, E):
                    ins = nc.vector.tensor_tensor(seen[:, :, e:e + 1], seen[:, :, e - 1:e], eq[:, :, e:e + 1], ALU.max)
                    if e < E - 1:
                        chain_c(ins)
                    else:
                        ins.then_inc(sem("seen_ready"), 1)
                dve.wait_ge(sem("seen_ready"), g + 1)
                nc.vector.tensor_copy(hot[:, :, 0:1], seen[:, :, 0:1]).then_inc(sem("hot_part"), 1)
                nc.vector.tensor_tensor(hot[:, :, 1:E], seen[:, :, 1:E], seen[:, :, 0:E - 1], ALU.subtract)\
                    .then_inc(sem("hot_part"), 1)
                dve.wait_ge(sem("hot_part"), g * 2 + 2)
                dve.wait_ge(sem("zs_ready"), g + 1)
                zv = zs[:].rearrange("p t (e r) -> p (t e) r", r=R)
                hv = hot[:].rearrange("p t e -> p (t e)").unsqueeze(2).broadcast_to([P, TILES * E, R])
                chain_c(nc.vector.tensor_tensor(zv, zv, hv, ALU.mult))
                def copies(t, n):
                    return t.unsqueeze(2).broadcast_to([P, TILES, n, E * R])

                prev(g, 1, 1, dve, sem("zt_ps_ready"))
                chain_c(nc.vector.tensor_copy(zp[:, :, 2:5], copies(zs[:], 3)))
                chain_c(nc.vector.tensor_tensor(zr[:], zs[:], zp[:, :, 2], ALU.subtract))
                chain_c(nc.vector.tensor_copy(zp[:, :, 0:2], copies(zr[:], 2)))
                nc.vector.tensor_tensor(zp[:, :, 5], zr[:], zp[:, :, 0], ALU.subtract)\
                    .then_inc(sem("zm_ready"), 1)

            def c_stats3(g):
                dve.wait_ge(sem("u_ready"), g * 2 + 2)
                stats(chain_c, h3, stats_c, mv_c, sem("stats_c_ready"))

            def c_out(g):
                c_norm(g, 3, h3, h3, sem("n3_ready"))
                for j in range(TILES):
                    dve.wait_ge(sem("n3_ready"), g * 2 + j + 1)
                    nc.vector.tensor_tensor(h3[:, j], h3[:, j], x1[:, j], ALU.add).then_inc(sem("out_ready"), 1)

            A_AT = {1: lambda g: a_t1(g), 2: lambda g: a_conv(g, 0), 3: lambda g: (a_conv(g, 1), a_dtv(g)),
                    4: lambda g: a_conv(g, 2), 5: lambda g: (a_dt(g), a_h0(g)),
                    7: lambda g: (a_dec(g, 0), a_dec(g, 1), a_att(g, 0)), 8: lambda g: a_att(g, 1),
                    9: lambda g: (a_y(g, 0), a_y(g, 1)), 10: lambda g: a_h1(g, 0), 11: lambda g: a_h1(g, 1),
                    12: lambda g: (a_h2(g, 0), a_h2(g, 1))}
            C_AT = {1: lambda g: c_x1(g), 2: lambda g: c_stats2(g), 3: lambda g: c_h3(g), 4: lambda g: c_t3(g, 0),
                    5: lambda g: c_t3(g, 1), 6: lambda g: c_route(g), 9: lambda g: c_stats3(g),
                    10: lambda g: c_out(g)}

            def step(a, b, c):
                if isinstance(a, int) and a == 0:
                    dve.wait_ge(masks_made, 9)
                    chain_a.group(0)
                    a_stats(0)
                    dve.wait_ge(small_loaded, 64)
                    ln_row(0)
                    a_center(0)
                    a_norm(0)
                    ln_row(1)
                if c is not None:
                    chain_c.group(c)
                if a is not None and not (isinstance(a, int) and a == 0):
                    chain_a.group(a)
                    a_stats(a)
                for f in range(FBLK):
                    if isinstance(a, int) and a <= 1:
                        prepare(a, f)
                    if b is not None:
                        b_prod(b, f)
                        b_lo(b, f)
                    if f == 0:
                        if a is not None and not (isinstance(a, int) and a == 0):
                            a_center(a)
                            a_norm(a)
                        if c is not None:
                            c_stats1(c)
                    if a is not None and f in A_AT:
                        A_AT[f](a)
                    if c is not None and f in C_AT:
                        C_AT[f](c)
                if a is not None:
                    a_t2(a)
                    chain_a.close()
                if b is not None:
                    b_mlp(b)
                if c is not None:
                    chain_c.close()

            steps(dve, step)

        @block.tensor
        def _(pe):
            def mm(dst, left, right, start, stop):
                return nc.tensor.matmul(dst, left, right, start=start, stop=stop)

            PAIRS = [(0, 0), (0, 1), (1, 0)]

            def split_product(dst, lefts, rights, start=True, stop=True):
                todo = [(lf[a], rt[b]) for lf, rt in zip(lefts, rights) for a, b in PAIRS]
                for n, (lf, rt) in enumerate(todo):
                    last = mm(dst, lf, rt, start and n == 0, stop and n == len(todo) - 1)
                return last

            def weight(u, k):
                return [Wh[:, u, s, k * P:(k + 1) * P] for s in range(2)]

            def tokens(t, k, j=None):
                q = slice(0, SEQ) if j is None else slice(j * P, j * P + P)
                return [t[:, s, k, q] for s in range(2)]

            def transposed(src, bank, b, ready):
                for k in range(2):
                    for j in range(TILES):
                        last = nc.tensor.transpose(bank[:, k * SEQ + j * P:k * SEQ + (j + 1) * P],
                                                   src[:, j, (2 * b + k) * P:(2 * b + k + 1) * P], ident[:])
                last.then_inc(ready, 1)

            def prepare(step, f):
                for kind, t, n in in_order.get((step, f), []):
                    if kind != "gram":
                        continue
                    a, b = PIECES[n]
                    m = piece_order.index(n)
                    pe.wait_ge(s_piece[n], 16)
                    if m >= 4:
                        pe.wait_ge(sem("gram_read"), m - 3)
                    for u in range(a, b):
                        for k in range(KB):
                            v = upper(W[:, u])[:, k * P:(k + 1) * P]
                            last = mm(gram_bank(m)[:, (u - a) * P:(u - a + 1) * P], v, v, k == 0, k == KB - 1)
                    last.then_inc(sem("gram_ready"), 1)

            def a_t1(g):
                pe.wait_ge(sem("hn_ready"), g * 2 + 2)
                for b in range(2):
                    if b == 0:
                        prev(g, 2, 2, pe, sem("h1_ready"))
                    prev(g, 2, 1, pe, sem("h2t_ready"))
                    transposed(hn, WA[b], b, sem("ht_ps_ready"))

            def channels(g, units, bank, ready):
                for m, u in enumerate(units):
                    if isinstance(g, int) and g == 0:
                        wait_split(pe, [u])
                    last = split_product(bank[:, m * SEQ:(m + 1) * SEQ], [weight(u, k) for k in range(KB)],
                                         [tokens(ht, k) for k in range(KB)])
                last.then_inc(ready, 1)

            def a_in(g, b):
                pe.wait_ge(sem("ht_ready"), g * 2 + 2)
                if b == 0:
                    prev(g, 2, 2, pe, sem("h2t_ready"))
                channels(g, (2 * b, 2 * b + 1), WA[[2, 0, 1][b]], sem("xbc_ps_ready"))

            def a_dt(g):
                pe.wait_ge(sem("pad_ready"), g * 3 + 1)
                if isinstance(g, int) and g == 0:
                    pe.wait_ge(small_split, 1)
                for j in range(TILES):
                    last = split_product(WA[2][:, j * H:(j + 1) * H], [tokens(ht, k, j) for k in range(KB)],
                                         [[dt_w[:, s, k] for s in range(2)] for k in range(KB)])
                last.then_inc(sem("dt_ps_ready"), 1)

            def a_z(g, b):
                pe.wait_ge(sem("pad_ready"), g * 3 + 2 + b)
                channels(g, (6 + 2 * b, 7 + 2 * b), WA[b], sem("z_ps_ready"))

            def a_tok(g):
                pe.wait_ge(sem("xbc_ready"), g * 3 + 1)
                pe.wait_ge(sem("dtv_ready"), g + 1)
                for n, (c, j) in enumerate([(0, 0), (0, 1), (1, 0)]):
                    last = nc.tensor.transpose(WA[2][:, n * P:(n + 1) * P], xbc[:, c, j * P:(j + 1) * P], ident[:])
                last.then_inc(sem("tok_ps_ready"), 1)

            def flat(t):
                return t.rearrange("p h q -> p (h q)")

            def a_dec(g, n):
                if n < TILES:
                    pe.wait_ge(sem("sz_ready"), g * 2 + n + 1)
                    pe.wait_ge(sem("ra_ready"), g * 2 + n + 1)
                else:
                    pe.wait_ge(sem("exp_ready"), g * 3 + 1)
                mm(WA[[0, 1, 0][n]][:], (below if n < TILES else ones)[:], flat(ra[:, min(n, 1)]), True, True)\
                    .then_inc(sem("dec_ps_ready"), 1)

            def a_att(g, j):
                if j == 0:
                    pe.wait_ge(sem("tok_ready"), g + 1)
                    pe.wait_ge(sem("xbc_ready"), g * 3 + 3)
                else:
                    pe.wait_ge(sem("exp_ready"), g * 3 + 2)
                q = slice(j * P, j * P + P)
                mm(WA[[2, 1][j]][:], xbc[:, 1, q], xbc[:, 2:6, q], True, True)\
                    .then_inc(sem("att_ps_ready"), 1)

            def a_state(g):
                pe.wait_ge(sem("attw_ready"), g * 2 + 1)
                pe.wait_ge(sem("xw_ready"), g + 1)
                mm(WA[2][:], tok[:, 2], flat(xw[:]), True, True).then_inc(sem("st_ps_ready"), 1)

            def a_y(g, j):
                if j == 0:
                    pe.wait_ge(sem("exp_ready"), g * 3 + 3)
                    mm(WA[0][:], tok[:, 0], flat(dec[:, 0]), True, True).then_inc(sem("y_ps_ready"), 1)
                else:
                    pe.wait_ge(sem("attw_ready"), g * 2 + 2)
                    pe.wait_ge(sem("state_ready"), g + 1)
                    pe.wait_ge(sem("ce_ready"), g + 1)
                    mm(WA[1][:], tok[:, 1], flat(dec[:, 1]), True, False)
                    for h in range(H):
                        last = mm(WA[1][:, h * P:(h + 1) * P], xw[:, h], ce[:, h], False, h == H - 1)
                    last.then_inc(sem("y_ps_ready"), 1)

            def a_o(g, j):
                pe.wait_ge(sem("y_ready"), g * 2 + j + 1)
                if j == 0:
                    pe.wait_ge(sem("state_ready"), g + 1)
                bank = WA[[2, 0][j]]
                for k in range(KB):
                    last = mm(bank[:], y[:, k, j * P:(j + 1) * P], W[:, U_OUT + k], k == 0, k == KB - 1)
                last.then_inc(sem("o_ps_ready"), 1)

            def a_t2(g):
                pe.wait_ge(sem("h2_ready"), g * 2 + 2)
                for b in range(2):
                    if b == 0:
                        pe.wait_ge(sem("y_ready"), g * 2 + 2)
                    transposed(hn, WA[1 + b], b, sem("h2t_ps_ready"))

            def b_gu(g, f):
                if f == 0:
                    pe.wait_ge(sem("h2t_ready"), g * 2 + 1)
                if f >= 2:
                    pe.wait_ge(sem("prod_ready"), g * FBLK + f - 1)
                else:
                    prev(g, FBLK, FBLK - 1 + f, pe, sem("prod_ready"))
                for m, base in enumerate((U_GATE, U_UP)):
                    if isinstance(g, int) and g == 0:
                        wait_split(pe, [base + f])
                    for ks in (0, 1), (2, 3):
                        if f == 0 and m == 0 and ks[0] == 2:
                            pe.wait_ge(sem("h2t_ready"), g * 2 + 2)
                        last = split_product(GU[f % 2][:, m * SEQ:(m + 1) * SEQ],
                                             [weight(base + f, k) for k in ks], [tokens(h2t, k) for k in ks],
                                             start=ks[0] == 0, stop=ks[-1] == KB - 1)
                last.then_inc(sem("gu_ready"), 1)

            def b_down(g, f):
                if f == 0:
                    prev(g, 2, 2, pe, sem("mlp_ready"))
                pe.wait_ge(sem("act_ready"), g * FBLK + f + 1)
                if isinstance(g, int) and g == 0:
                    wait_split(pe, [U_DOWN + f])
                for j in range(TILES):
                    left = [act[:, slot(f), s, j * P:(j + 1) * P] for s in range(2)]
                    last = split_product(ACC[j][:], [left], [[Wh[:, U_DOWN + f, s] for s in range(2)]],
                                         start=f == 0, stop=f == FBLK - 1)
                    if f == FBLK - 1 and j == 0:
                        last.then_inc(sem("acc0_ready"), 1)
                last.then_inc(sem("down_done"), 1)

            def c_t3(g, b):
                if b == 0:
                    pe.wait_ge(sem("h3_ready"), g * 2 + 2)
                    prev(g, 2, 2, pe, sem("u_ready"))
                elif alone(g):
                    pe.wait_ge(sem("prod_ready"), g * FBLK + FBLK)
                else:
                    pe.wait_ge(sem("h3t_ready"), g * 2 + 1)
                transposed(h3, h3t_bank(g, b), b, sem("h3t_ps_ready"))

            def c_logits(g):
                pe.wait_ge(sem("h3t_ready"), g * 2 + 2)
                n = E + E * R
                for j in range(TILES):
                    last = split_product(WC[:, j * n:(j + 1) * n], [tokens(h3t, k, j) for k in range(KB)],
                                         [[gl_w[:, s, k] for s in range(2)] for k in range(KB)])
                last.then_inc(sem("lg_ps_ready"), 1)

            def c_zt(g):
                if alone(g):
                    c_linear(g, 0)
                pe.wait_ge(sem("zm_ready"), g + 1)
                bank = WC[:].bitcast(BF16)
                for j in range(TILES):
                    q = slice(j * P, (j + 1) * P)
                    nc.tensor.transpose(bank[:, q], zp[:, j, 0:4].rearrange("p n r -> p (n r)"), upper(ident[:]))
                    last = nc.tensor.transpose(bank[0:2 * E * R, SEQ:2 * SEQ][:, q],
                                               zp[:, j, 4:6].rearrange("p n r -> p (n r)"), upper(ident[:]))
                last.then_inc(sem("zt_ps_ready"), 1)
                if alone(g):
                    c_linear(g, 1)

            def c_linear(g, j):
                if alone(g):
                    pe.wait_ge(sem("mlp_ready"), g * 2 + 2)
                split_product(u_bank(g, j)[:], [tokens(h3t, k, j) for k in range(KB)],
                              [[Wh[:, U_LIN + k, s] for s in range(2)] for k in range(KB)], stop=False)

            def c_lora(g, j):
                mm(u_bank(g, j)[:], zt_1[:, j * P:(j + 1) * P], lora_1[:], False, False)
                mm(u_bank(g, j)[:], zt_2[:, j * P:(j + 1) * P], lora_2[:], False, True)\
                    .then_inc(sem("u_ps_ready"), 1)

            def c_u(g, j):
                if alone(g):
                    pe.wait_ge(sem("zt_ready"), g * 2 + 2)
                elif j == 0:
                    pe.wait_ge(sem("zt_ready"), g * 2 + 2)
                    c_linear(g, j)
                else:
                    pe.wait_ge(sem("u_ready"), g * 2 + 1)
                    c_linear(g, j)
                c_lora(g, j)

            A_AT = {1: lambda g: a_t1(g), 2: lambda g: a_in(g, 0), 3: lambda g: (a_in(g, 1), a_in(g, 2), a_dt(g)),
                    4: lambda g: a_z(g, 0), 5: lambda g: (a_z(g, 1), a_tok(g)),
                    6: lambda g: (a_dec(g, 0), a_dec(g, 1)), 7: lambda g: (a_att(g, 0), a_dec(g, 2)),
                    8: lambda g: (a_att(g, 1), a_state(g)), 9: lambda g: (a_y(g, 0), a_y(g, 1)),
                    10: lambda g: a_o(g, 0), 11: lambda g: a_o(g, 1), 13: lambda g: a_t2(g)}
            C_AT = {4: lambda g: c_t3(g, 0), 5: lambda g: c_t3(g, 1), 6: lambda g: c_logits(g),
                    7: lambda g: c_zt(g), 8: lambda g: c_u(g, 0), 9: lambda g: c_u(g, 1)}

            def step(a, b, c):
                if isinstance(a, int) and a == 0:
                    pe.wait_ge(masks_made, 9)
                for f in range(FBLK):
                    if isinstance(a, int) and a <= 1:
                        prepare(a, f)
                    if isinstance(b, int) and b == 0 and f == 0:
                        pe.wait_ge(sem("gram_read"), len(piece_order) - 1)
                    if isinstance(a, int) and a == 0 and f == 10:
                        pe.wait_ge(s_piece[piece_of(U_OUT)], 16)
                    if isinstance(c, int) and c == 0 and f == 4:
                        wait_split(pe, UNITS_OF[T_LIN])
                        pe.wait_ge(small_split, 2)
                        pe.wait_ge(sem("lora_split"), 2)
                    if b is not None:
                        b_gu(b, f)
                        if f:
                            b_down(b, f - 1)
                    if a is not None and f in A_AT:
                        A_AT[f](a)
                    if c is not None and f in C_AT:
                        C_AT[f](c)
                if b is not None:
                    b_down(b, FBLK - 1)

            steps(pe, step)


RING = 4


def slot(f):
    return f % RING


def last_in_slot(f):
    return max(b for b in range(FBLK) if slot(b) == slot(f))


_OUT = (2048, 512)


def kernel(**inputs):
    import numpy as np
    import concourse.bacc as bacc
    from concourse.bass_utils import run_bass_kernel_spmd

    a = {n.replace("L0_", ""): np.asarray(v) for n, v in inputs.items()}

    def by_output(w, blocks):
        return w.reshape(blocks, P, KB, P).transpose(0, 3, 2, 1)

    w_in = a["attn_w_in"]
    z_rows, xbc_rows, dt_rows = np.split(w_in, [H * P, H * P + XBC * P])
    gl = np.concatenate([a["ffn_gate_w"], a["ffn_lora_A"].reshape(E * R, D)])
    arrays = {
        "x": a["attn_hidden_states"].reshape(-1, D),
        "w_in": by_output(np.concatenate([xbc_rows, z_rows]), XBC + H),
        "w_dt": dt_rows.T.reshape(KB, P, H).transpose(1, 0, 2),
        "w_out": a["attn_w_out"].T.reshape(KB, P, D),
        "w_gate": by_output(a["attn_gate_w"], FBLK),
        "w_up": by_output(a["attn_up_w"], FBLK),
        "w_down": a["attn_down_w"].T.reshape(FBLK, P, D),
        "w_lin": a["ffn_W_up"].T.reshape(KB, P, D),
        "w_gl": gl.T.reshape(KB, P, E + E * R).transpose(1, 0, 2),
        "lora_b": np.tile(a["ffn_lora_B"].transpose(0, 2, 1).reshape(E * R, D), (4, 1)),
        "cols": np.concatenate([a["attn_conv_w"].reshape(XBC, P, TAPS).transpose(1, 0, 2).reshape(P, -1),
                                a["attn_conv_b"].reshape(XBC, P).T], axis=1),
        "rows": np.concatenate([a["attn_A_log"], a["attn_D"], a["attn_dt_bias"],
                                a["ffn_expert_bias"]])[None, :],
        "ln_rows": np.concatenate([a["attn_ln1_w"], a["attn_ln2_w"]])[None, :],
    }
    arrays = {f"in_{n}": np.ascontiguousarray(v) for n, v in arrays.items()}
    nc = bacc.Bacc("TRN2", target_bir_lowering=False, num_devices=1)
    args = [nc.dram_tensor(n, v.shape, mybir.dt.from_np(v.dtype), kind="ExternalInput").ap()
            for n, v in arrays.items()]
    out = nc.dram_tensor("out_x", _OUT, F32, kind="ExternalOutput").ap()
    build(nc, *args, out)
    r = run_bass_kernel_spmd(nc, [arrays], core_ids=[0])
    return r.results[0]["out_x"].reshape(a["attn_hidden_states"].shape)
```
